# Optimizing a Trainium2 kernel written in Bass

```python
import numpy as np
import jax
import jax.numpy as jnp

def _softmax(x, axis=-1):
    return jax.nn.softmax(x, axis=axis)

def _gelu(x):
    return jax.nn.gelu(x, approximate=True)

def _silu(x):
    return jax.nn.silu(x)

def _sigmoid(x):
    return jax.nn.sigmoid(x)

def _layernorm(x, axis=-1, eps=1e-05):
    m = jnp.mean(x, axis=axis, keepdims=True)
    v = jnp.var(x, axis=axis, keepdims=True)
    return (x - m) / jnp.sqrt(v + eps)

def _scatter_add(tgt, idx, src, axis=0):
    return tgt.at[idx].add(src)

def _segment_sum(src, seg, n):
    return jax.ops.segment_sum(src, seg, n)
kernel_name = 'mk_dlrm_tower_d1_rec_r8_ce9ed8'

def setup_inputs(seed: int=0):
    np.random.seed(seed)
    _w = jnp.asarray

    def _rec_inputs():
        import jax
        import jax.numpy as jnp
        _tk = jax.random.key(seed)
        dense_ctx = jax.random.normal(jax.random.fold_in(_tk, 190), (1024, 16), jnp.float32)
        ids = jnp.stack([jax.random.randint(jax.random.fold_in(_tk, 200 + f), (1024,), 0, v, jnp.int32) for f, v in enumerate([1250, 12500, 12500, 125000, 1000, 1000, 12500, 12500, 125000, 1000, 1250, 1000, 1000, 1250, 125000, 1250, 125000, 1000, 1000, 125000, 12500, 125000, 12500, 12500, 1250, 1250, 12500, 125000, 1000, 125000, 1250, 1250, 125000, 1250, 1250, 12500, 125000, 12500, 12500])], axis=1)
        tbl_0 = 0.05 * jax.random.normal(jax.random.fold_in(_tk, 500 + 0), (1250, 16), jnp.float32)
        tbl_1 = 0.05 * jax.random.normal(jax.random.fold_in(_tk, 500 + 1), (12500, 16), jnp.float32)
        tbl_2 = 0.05 * jax.random.normal(jax.random.fold_in(_tk, 500 + 2), (12500, 16), jnp.float32)
        tbl_3 = 0.05 * jax.random.normal(jax.random.fold_in(_tk, 500 + 3), (125000, 16), jnp.float32)
        tbl_4 = 0.05 * jax.random.normal(jax.random.fold_in(_tk, 500 + 4), (1000, 16), jnp.float32)
        tbl_5 = 0.05 * jax.random.normal(jax.random.fold_in(_tk, 500 + 5), (1000, 16), jnp.float32)
        tbl_6 = 0.05 * jax.random.normal(jax.random.fold_in(_tk, 500 + 6), (12500, 16), jnp.float32)
        tbl_7 = 0.05 * jax.random.normal(jax.random.fold_in(_tk, 500 + 7), (12500, 16), jnp.float32)
        tbl_8 = 0.05 * jax.random.normal(jax.random.fold_in(_tk, 500 + 8), (125000, 16), jnp.float32)
        tbl_9 = 0.05 * jax.random.normal(jax.random.fold_in(_tk, 500 + 9), (1000, 16), jnp.float32)
        tbl_10 = 0.05 * jax.random.normal(jax.random.fold_in(_tk, 500 + 10), (1250, 16), jnp.float32)
        tbl_11 = 0.05 * jax.random.normal(jax.random.fold_in(_tk, 500 + 11), (1000, 16), jnp.float32)
        tbl_12 = 0.05 * jax.random.normal(jax.random.fold_in(_tk, 500 + 12), (1000, 16), jnp.float32)
        tbl_13 = 0.05 * jax.random.normal(jax.random.fold_in(_tk, 500 + 13), (1250, 16), jnp.float32)
        tbl_14 = 0.05 * jax.random.normal(jax.random.fold_in(_tk, 500 + 14), (125000, 16), jnp.float32)
        tbl_15 = 0.05 * jax.random.normal(jax.random.fold_in(_tk, 500 + 15), (1250, 16), jnp.float32)
        tbl_16 = 0.05 * jax.random.normal(jax.random.fold_in(_tk, 500 + 16), (125000, 16), jnp.float32)
        tbl_17 = 0.05 * jax.random.normal(jax.random.fold_in(_tk, 500 + 17), (1000, 16), jnp.float32)
        tbl_18 = 0.05 * jax.random.normal(jax.random.fold_in(_tk, 500 + 18), (1000, 16), jnp.float32)
        tbl_19 = 0.05 * jax.random.normal(jax.random.fold_in(_tk, 500 + 19), (125000, 16), jnp.float32)
        tbl_20 = 0.05 * jax.random.normal(jax.random.fold_in(_tk, 500 + 20), (12500, 16), jnp.float32)
        tbl_21 = 0.05 * jax.random.normal(jax.random.fold_in(_tk, 500 + 21), (125000, 16), jnp.float32)
        tbl_22 = 0.05 * jax.random.normal(jax.random.fold_in(_tk, 500 + 22), (12500, 16), jnp.float32)
        tbl_23 = 0.05 * jax.random.normal(jax.random.fold_in(_tk, 500 + 23), (12500, 16), jnp.float32)
        tbl_24 = 0.05 * jax.random.normal(jax.random.fold_in(_tk, 500 + 24), (1250, 16), jnp.float32)
        tbl_25 = 0.05 * jax.random.normal(jax.random.fold_in(_tk, 500 + 25), (1250, 16), jnp.float32)
        tbl_26 = 0.05 * jax.random.normal(jax.random.fold_in(_tk, 500 + 26), (12500, 16), jnp.float32)
        tbl_27 = 0.05 * jax.random.normal(jax.random.fold_in(_tk, 500 + 27), (125000, 16), jnp.float32)
        tbl_28 = 0.05 * jax.random.normal(jax.random.fold_in(_tk, 500 + 28), (1000, 16), jnp.float32)
        tbl_29 = 0.05 * jax.random.normal(jax.random.fold_in(_tk, 500 + 29), (125000, 16), jnp.float32)
        tbl_30 = 0.05 * jax.random.normal(jax.random.fold_in(_tk, 500 + 30), (1250, 16), jnp.float32)
        tbl_31 = 0.05 * jax.random.normal(jax.random.fold_in(_tk, 500 + 31), (1250, 16), jnp.float32)
        tbl_32 = 0.05 * jax.random.normal(jax.random.fold_in(_tk, 500 + 32), (125000, 16), jnp.float32)
        tbl_33 = 0.05 * jax.random.normal(jax.random.fold_in(_tk, 500 + 33), (1250, 16), jnp.float32)
        tbl_34 = 0.05 * jax.random.normal(jax.random.fold_in(_tk, 500 + 34), (1250, 16), jnp.float32)
        tbl_35 = 0.05 * jax.random.normal(jax.random.fold_in(_tk, 500 + 35), (12500, 16), jnp.float32)
        tbl_36 = 0.05 * jax.random.normal(jax.random.fold_in(_tk, 500 + 36), (125000, 16), jnp.float32)
        tbl_37 = 0.05 * jax.random.normal(jax.random.fold_in(_tk, 500 + 37), (12500, 16), jnp.float32)
        tbl_38 = 0.05 * jax.random.normal(jax.random.fold_in(_tk, 500 + 38), (12500, 16), jnp.float32)
        _rk = jax.random.fold_in(_tk, 7)
        W_top1 = 0.05 * jax.random.normal(jax.random.fold_in(_tk, 801), (400, 512), jnp.float32)
        W_top2 = 0.0441942 * jax.random.normal(jax.random.fold_in(_tk, 802), (512, 256), jnp.float32)
        W_top3 = 0.0625 * jax.random.normal(jax.random.fold_in(_tk, 803), (256, 1), jnp.float32)
        b_top1 = jnp.zeros((512,), jnp.float32)
        b_top2 = jnp.zeros((256,), jnp.float32)
        return (dense_ctx, ids, tbl_0, tbl_1, tbl_2, tbl_3, tbl_4, tbl_5, tbl_6, tbl_7, tbl_8, tbl_9, tbl_10, tbl_11, tbl_12, tbl_13, tbl_14, tbl_15, tbl_16, tbl_17, tbl_18, tbl_19, tbl_20, tbl_21, tbl_22, tbl_23, tbl_24, tbl_25, tbl_26, tbl_27, tbl_28, tbl_29, tbl_30, tbl_31, tbl_32, tbl_33, tbl_34, tbl_35, tbl_36, tbl_37, tbl_38, W_top1, b_top1, W_top2, b_top2, W_top3)
    dense_ctx, ids, tbl_0, tbl_1, tbl_2, tbl_3, tbl_4, tbl_5, tbl_6, tbl_7, tbl_8, tbl_9, tbl_10, tbl_11, tbl_12, tbl_13, tbl_14, tbl_15, tbl_16, tbl_17, tbl_18, tbl_19, tbl_20, tbl_21, tbl_22, tbl_23, tbl_24, tbl_25, tbl_26, tbl_27, tbl_28, tbl_29, tbl_30, tbl_31, tbl_32, tbl_33, tbl_34, tbl_35, tbl_36, tbl_37, tbl_38, W_top1, b_top1, W_top2, b_top2, W_top3 = _rec_inputs()

    def _L0_rec_setup():
        import jax, jax.numpy as jnp
        import numpy as np
        B, F0, D = (512, 39, 16)
        CIN = [128, 128, 128]

        def _cin_layer(X0, Xi, W, b):
            H = W.shape[0]
            F0_, Fi = (X0.shape[1], Xi.shape[1])
            Wr = W.reshape(H, F0_, Fi)
            return jnp.einsum('hjk,bjd,bkd->bhd', Wr, X0, Xi) + b[None, :, None]
        key = jax.random.key(seed)
        ks = jax.random.split(key, 4)
        x = jax.random.normal(ks[0], (B, F0, D), dtype=jnp.float32)
        fields = [F0] + CIN
        inp = {'embedded_features': x}
        for i in range(len(CIN)):
            cin = F0 * fields[i]
            cout = fields[i + 1]
            kw = jax.random.fold_in(ks[1], i)
            inp[f'W{i}'] = jax.random.normal(kw, (cout, cin), dtype=jnp.float32) / np.sqrt(cin)
            inp[f'b{i}'] = jnp.zeros((cout,), dtype=jnp.float32)
        return inp
    _L0_rec_all = _L0_rec_setup()
    _L0_rec_in = {k: v for k, v in _L0_rec_all.items() if k in ('W0', 'b0', 'W1', 'b1', 'W2', 'b2')}
    del _L0_rec_all
    return {'dense_ctx': dense_ctx, 'ids': ids, 'tbl_0': tbl_0, 'tbl_1': tbl_1, 'tbl_2': tbl_2, 'tbl_3': tbl_3, 'tbl_4': tbl_4, 'tbl_5': tbl_5, 'tbl_6': tbl_6, 'tbl_7': tbl_7, 'tbl_8': tbl_8, 'tbl_9': tbl_9, 'tbl_10': tbl_10, 'tbl_11': tbl_11, 'tbl_12': tbl_12, 'tbl_13': tbl_13, 'tbl_14': tbl_14, 'tbl_15': tbl_15, 'tbl_16': tbl_16, 'tbl_17': tbl_17, 'tbl_18': tbl_18, 'tbl_19': tbl_19, 'tbl_20': tbl_20, 'tbl_21': tbl_21, 'tbl_22': tbl_22, 'tbl_23': tbl_23, 'tbl_24': tbl_24, 'tbl_25': tbl_25, 'tbl_26': tbl_26, 'tbl_27': tbl_27, 'tbl_28': tbl_28, 'tbl_29': tbl_29, 'tbl_30': tbl_30, 'tbl_31': tbl_31, 'tbl_32': tbl_32, 'tbl_33': tbl_33, 'tbl_34': tbl_34, 'tbl_35': tbl_35, 'tbl_36': tbl_36, 'tbl_37': tbl_37, 'tbl_38': tbl_38, 'W_top1': W_top1, 'b_top1': b_top1, 'W_top2': W_top2, 'b_top2': b_top2, 'W_top3': W_top3, 'L0_rec_W0': _L0_rec_in['W0'], 'L0_rec_b0': _L0_rec_in['b0'], 'L0_rec_W1': _L0_rec_in['W1'], 'L0_rec_b1': _L0_rec_in['b1'], 'L0_rec_W2': _L0_rec_in['W2'], 'L0_rec_b2': _L0_rec_in['b2']}

def reference(dense_ctx, ids, tbl_0, tbl_1, tbl_2, tbl_3, tbl_4, tbl_5, tbl_6, tbl_7, tbl_8, tbl_9, tbl_10, tbl_11, tbl_12, tbl_13, tbl_14, tbl_15, tbl_16, tbl_17, tbl_18, tbl_19, tbl_20, tbl_21, tbl_22, tbl_23, tbl_24, tbl_25, tbl_26, tbl_27, tbl_28, tbl_29, tbl_30, tbl_31, tbl_32, tbl_33, tbl_34, tbl_35, tbl_36, tbl_37, tbl_38, W_top1, b_top1, W_top2, b_top2, W_top3, L0_rec_W0, L0_rec_b0, L0_rec_W1, L0_rec_b1, L0_rec_W2, L0_rec_b2):
    import jax
    import jax.numpy as jnp

    def _L0_rec_ref(embedded_features, W0, b0, W1, b1, W2, b2):
        import jax, jax.numpy as jnp
        import numpy as np
        B, F0, D = (512, 39, 16)
        CIN = [128, 128, 128]

        def _cin_layer(X0, Xi, W, b):
            H = W.shape[0]
            F0_, Fi = (X0.shape[1], Xi.shape[1])
            Wr = W.reshape(H, F0_, Fi)
            return jnp.einsum('hjk,bjd,bkd->bhd', Wr, X0, Xi) + b[None, :, None]
        X0 = embedded_features
        Ws = [(W0, b0), (W1, b1), (W2, b2)]
        Xi = X0
        res = []
        for W, b in Ws:
            Xi = _cin_layer(X0, Xi, W, b)
            res.append(Xi.sum(axis=2))
        return jnp.concatenate(res, axis=1)
    e = jnp.stack([tbl_0[ids[:, 0]], tbl_1[ids[:, 1]], tbl_2[ids[:, 2]], tbl_3[ids[:, 3]], tbl_4[ids[:, 4]], tbl_5[ids[:, 5]], tbl_6[ids[:, 6]], tbl_7[ids[:, 7]], tbl_8[ids[:, 8]], tbl_9[ids[:, 9]], tbl_10[ids[:, 10]], tbl_11[ids[:, 11]], tbl_12[ids[:, 12]], tbl_13[ids[:, 13]], tbl_14[ids[:, 14]], tbl_15[ids[:, 15]], tbl_16[ids[:, 16]], tbl_17[ids[:, 17]], tbl_18[ids[:, 18]], tbl_19[ids[:, 19]], tbl_20[ids[:, 20]], tbl_21[ids[:, 21]], tbl_22[ids[:, 22]], tbl_23[ids[:, 23]], tbl_24[ids[:, 24]], tbl_25[ids[:, 25]], tbl_26[ids[:, 26]], tbl_27[ids[:, 27]], tbl_28[ids[:, 28]], tbl_29[ids[:, 29]], tbl_30[ids[:, 30]], tbl_31[ids[:, 31]], tbl_32[ids[:, 32]], tbl_33[ids[:, 33]], tbl_34[ids[:, 34]], tbl_35[ids[:, 35]], tbl_36[ids[:, 36]], tbl_37[ids[:, 37]], tbl_38[ids[:, 38]]], axis=1)
    z = _L0_rec_ref(e, L0_rec_W0, L0_rec_b0, L0_rec_W1, L0_rec_b1, L0_rec_W2, L0_rec_b2)
    z = z.reshape(z.shape[0], -1)
    h = jnp.concatenate([z, dense_ctx], axis=1)
    h = jnp.maximum(h @ W_top1 + b_top1, 0.0)
    h = jnp.maximum(h @ W_top2 + b_top2, 0.0)
    y = h @ W_top3
    return y

_drawn_inputs = setup_inputs


def setup_inputs(seed=0):
    import zlib

    import numpy as np

    out = dict(_drawn_inputs(seed))
    spreads = {'b_top1': (0.0, 0.1),
     'b_top2': (0.0, 0.1),
     'L0_rec_b0': (0.0, 0.1),
     'L0_rec_b1': (0.0, 0.1),
     'L0_rec_b2': (0.0, 0.1)}
    factors = {'tbl_0': 8.0,
     'tbl_1': 6.085,
     'tbl_2': 4.902,
     'tbl_3': 7.09,
     'tbl_4': 8.0,
     'tbl_5': 8.0,
     'tbl_6': 8.0,
     'tbl_7': 6.533,
     'tbl_8': 8.0,
     'tbl_9': 8.0,
     'tbl_10': 8.0,
     'tbl_11': 6.842,
     'tbl_12': 8.0,
     'tbl_13': 8.0,
     'tbl_14': 4.335,
     'tbl_15': 5.861,
     'tbl_16': 8.0,
     'tbl_17': 8.0,
     'tbl_18': 8.0,
     'tbl_19': 5.728,
     'tbl_20': 7.432,
     'tbl_21': 8.0,
     'tbl_22': 8.0,
     'tbl_23': 8.0,
     'tbl_24': 8.0,
     'tbl_25': 7.07,
     'tbl_26': 6.077,
     'tbl_27': 8.0,
     'tbl_28': 8.0,
     'tbl_29': 8.0,
     'tbl_30': 6.392,
     'tbl_31': 6.195,
     'tbl_32': 8.0,
     'tbl_33': 6.868,
     'tbl_34': 8.0,
     'tbl_35': 7.056,
     'tbl_36': 8.0,
     'tbl_37': 6.484,
     'tbl_38': 8.0,
     'L0_rec_W0': 3.255}
    for name, (base, spread) in spreads.items():
        noise = np.random.default_rng([zlib.crc32(name.encode()), seed]).standard_normal(out[name].shape)
        drawn = base * np.exp(spread * noise) if base else spread * noise
        out[name] = jnp.asarray(drawn.astype(out[name].dtype))
    for name, factor in factors.items():
        out[name] = (out[name] * factor).astype(out[name].dtype)
    return out
```

```python
from contextlib import ExitStack

import concourse.bass as bass
from concourse import mybir

P = 128
B, F, D, H = 1024, 39, 16, 128
TILES = B // P
GB = P // D
GPT = P // GB
SHIFTS = (F + 1) // 2
WRAP = F + SHIFTS - 1
PAIRS = SHIFTS * F
KT = -(-PAIRS // P)
KLAST = PAIRS - (KT - 1) * P
NDENSE, N1, N2 = 16, 512, 256
FJ = F + 1
JC = 4
CHUNKS = -(-F // JC)
HALF = CHUNKS // 2
SLOTS = 8
DVE_J = [j for c in range(1, CHUNKS, 2) for j in range(JC * c, min(JC * c + JC, F))]
STEPS = len(DVE_J)
POOL_STEPS = HALF
EARLY = 20
XT = 6

F32 = mybir.dt.float32
F32R = mybir.dt.float32r
I32 = mybir.dt.int32
ALU = mybir.AluOpType
ACT = mybir.ActivationFunctionType
AX_X = mybir.AxisListType.X


def wait(eng, sem, t, per_tile, n):
    if isinstance(t, int) and t * per_tile + n <= 0:
        return
    eng.wait_ge(sem, t * per_tile + n)


def chunk_j(c):
    return range(JC * c, min(JC * c + JC, F))


def dlrm_cin_kernel(nc, tables, ids, dense_t, w0a, w0b, b0, w1_t, b1, w2_t, b2,
                    wt1, bt1, wt2, bt2, wt3, identity, row_mask, out):
    ctx = ExitStack()
    with ctx:
        def sb(name, shape, dt=F32):
            return ctx.enter_context(nc.sbuf_tensor(name, shape, dt))

        def pb(name):
            return ctx.enter_context(nc.psum_tensor(name, [P, 512], F32))

        def sem(name):
            return ctx.enter_context(nc.semaphore(name))

        w1_raw = sb("w1_raw", [P, F * H])
        w1_hi = sb("w1_hi", [P, F * H], F32R)
        w1_lo = sb("w1_lo", [P, F * H], F32R)
        w2 = sb("w2", [P, F, H])
        w0 = sb("w0", [P, KT, H])
        w0_other = sb("w0_other", [P, KT, H])
        wt1_z = sb("wt1_z", [P, 3, N1])
        wt1_dense = sb("wt1_dense", [NDENSE, N1])
        wt2_sb = sb("wt2_sb", [P, N1 // P, N2])
        wt3_sb = sb("wt3_sb", [P, N2 // P])
        bt1_sb = sb("bt1_sb", [P, N1 // P])
        bt2_sb = sb("bt2_sb", [P, N2 // P])
        b0_sb = sb("b0_sb", [P, 1])
        b0_16 = sb("b0_16", [P, 1])
        b1_rows = sb("b1_rows", [P, H])
        b2_sb = sb("b2_sb", [P, 1])
        b2_16 = sb("b2_16", [P, 1])
        ident = sb("ident", [P, P])
        mask = sb("mask", [P, GB])
        dense = sb("dense", [NDENSE, B])
        ids_tile = sb("ids_tile", [P, F], I32)
        emb = sb("emb", [P, F * D])
        x_f = sb("x_f", [F, P, D])
        x_bd = sb("x_bd", [P, GPT, WRAP])
        x_now = sb("x_now", [P, 4, FJ])
        z = sb("z", [P, 2, PAIRS])
        z_t = sb("z_t", [P, 2, KT, P])
        x1_hi = sb("x1_hi", [P, 2, P], F32R)
        x1_lo = sb("x1_lo", [P, 2, P], F32R)
        scaled = sb("scaled", [P, SLOTS, JC * H])
        pool_sum = sb("pool_sum", [P, JC * H])
        parts = sb("parts", [P, 2, 4, H])
        x2 = sb("x2", [P, 2, H])
        x_diag = sb("x_diag", [P, 2, GB, FJ])
        g_sb = sb("g_sb", [P, FJ, P])
        res0 = sb("res0", [P, P])
        z_top = sb("z_top", [P, 3, P])
        h1 = sb("h1", [P, N1 // P, P])
        h2 = sb("h2", [P, N2 // P, P])
        y_sb = sb("y_sb", [1, P])

        y_act = [pb("y_act0"), pb("y_act1")]
        y_dve = [pb("y_dve0"), pb("y_dve1")]
        zt = pb("zt")
        cin0 = pb("cin0")[:, 0:P]
        g_ps = pb("g_ps")
        misc = pb("misc")

        s_ids = sem("ids_loaded")
        s_gather = sem("gathered")
        s_w1 = sem("w1_loaded")
        s_w0 = sem("w0_loaded")
        s_w2 = sem("w2_loaded")
        s_const = sem("consts_loaded")
        s_top = sem("top_loaded")
        s_ones = sem("ones_set")
        s_w1hi = sem("w1_hi_made")
        s_w1lo = sem("w1_lo_made")
        s_w0sum = sem("w0_summed")
        s_bias = sem("biases_made")
        s_xt = sem("x_transposed")
        s_xf = sem("x_f_written")
        s_xbd = sem("x_bd_written")
        s_z = sem("z_made")
        s_now = sem("x_now_made")
        s_zt = sem("z_transposed")
        s_ztc = sem("z_t_written")
        s_cin0 = sem("cin0_summed")
        s_x1hi = sem("x1_hi_made")
        s_x1lo = sem("x1_lo_made")
        s_res0 = sem("res0_made")
        s_yact = sem("y_for_act")
        s_ydve = sem("y_for_dve")
        s_scaled = sem("scaled")
        s_steps = sem("dve_steps")
        s_pool = sem("pool_steps")
        s_x2 = sem("x2_made")
        s_diag = sem("x_diag_made")
        s_g = sem("g_summed")
        s_gc = sem("g_written")
        s_cin2 = sem("cin2_summed")
        s_ztop0 = sem("z_top0_made")
        s_ztop1 = sem("z_top1_made")
        s_ztop2 = sem("z_top2_made")
        s_h1p = sem("h1_summed")
        s_h1 = sem("h1_made")
        s_h2p = sem("h2_summed")
        s_h2 = sem("h2_made")
        s_yp = sem("y_summed")
        s_y = sem("y_made")
        s_out = sem("y_stored")

        block = ctx.enter_context(nc.Block())

        def tiles(eng, body):
            body(0, True, False)
            with eng.Fori(1, TILES - 1) as t:
                body(t, False, False)
            body(TILES - 1, False, True)

        @block.sync
        def _(sp):
            def load_ids(t):
                wait(sp, s_gather, t, 16 * F, 0)
                sp.dma_start(ids_tile[:, :], ids[bass.ds(t * P, P), :]).then_inc(s_ids, 16)

            load_ids(0)
            sp.dma_start(ident[:, :], identity).then_inc(s_const, 16)
            sp.dma_start(mask[:, :], row_mask).then_inc(s_const, 16)
            sp.dma_start(b0_sb[:, :], b0).then_inc(s_const, 16)
            sp.dma_start(b2_sb[:, :], b2).then_inc(s_const, 16)
            sp.dma_start(b1_rows[:, :], bass.AP(b1.tensor, 0, [[0, P], [1, H]])).then_inc(s_const, 16)
            sp.dma_start(w0[:, :, :], w0a).then_inc(s_w0, 16)
            sp.dma_start(w0_other[:, :, :], w0b).then_inc(s_w0, 16)
            sp.dma_start(w1_raw[:, :], w1_t).then_inc(s_w1, 16)
            sp.dma_start(w2[:, :, :], w2_t).then_inc(s_w2, 16)
            sp.dma_start(wt1_z[:, :, :], wt1[0:3 * H, :].rearrange("(l p) n -> p l n", p=P)).then_inc(s_top, 16)
            sp.dma_start(wt1_dense[:, :], wt1[3 * H:3 * H + NDENSE, :]).then_inc(s_top, 16)
            sp.dma_start(wt2_sb[:, :, :], wt2.rearrange("(l p) n -> p l n", p=P)).then_inc(s_top, 16)
            sp.dma_start(wt3_sb[:, :], wt3).then_inc(s_top, 16)
            sp.dma_start(bt1_sb[:, :], bt1).then_inc(s_top, 16)
            sp.dma_start(bt2_sb[:, :], bt2).then_inc(s_top, 16)
            sp.dma_start(dense[:, :], dense_t).then_inc(s_top, 16)

            def store(t):
                wait(sp, s_y, t, 1, 1)
                sp.dma_start(out[:, bass.ds(t * P, P)], y_sb[:, :]).then_inc(s_out, 16)

            load_ids(1)
            load_ids(2)
            with sp.Fori(1, TILES - 1) as t:
                load_ids(t + 2)
                store(t - 1)
            store(TILES - 2)
            store(TILES - 1)
            sp.wait_ge(s_out, 16 * TILES)

        @block.gpsimd
        def _(pool):
            def gather(t, fields):
                for f in fields:
                    nc.gpsimd.indirect_dma_start(
                        out=emb[:, f * D:(f + 1) * D], out_offset=None, in_=tables[f],
                        in_offset=bass.IndirectOffsetOnAxis(ap=ids_tile[:, f:f + 1], axis=0),
                    ).then_inc(s_gather, 16)

            def gather_waits(t):
                wait(pool, s_ids, t, 16, 16)
                wait(pool, s_xt, t, XT, -2)

            def add(t, n, out_, a, b):
                wait(pool, s_pool, t, GPT * POOL_STEPS, n)
                nc.gpsimd.tensor_tensor(out_, a, b, ALU.add).then_inc(s_pool, 1)

            def body(t, first, last):
                for i in range(GPT):
                    n = POOL_STEPS * i
                    for m in range(1, HALF):
                        wait(pool, s_scaled, t, GPT * HALF, HALF * i + m + 1)
                        slot = (HALF * i + m) % SLOTS
                        add(t, n + m - 1, pool_sum[:, :], scaled[:, (slot - 1) % SLOTS, :] if m == 1 else pool_sum[:, :],
                            scaled[:, slot, :])
                    if (i == 0 and first) or (i == 9 and not last):
                        gather_waits(t + 1 if i == 0 else t + 2)
                    wait(pool, s_x2, t, GPT, i - 1)
                    add(t, n + HALF - 1, parts[:, i % 2, 2:4, :], pool_sum[:, 0:2 * H], pool_sum[:, 2 * H:4 * H])
                    if first:
                        gather(t + 1, range(6 * i, min(6 * i + 6, F)))
                    elif not last:
                        gather(t + 1, range(EARLY + 3 * i, min(EARLY + 3 * i + 3, F)))
                    if i >= 9 and not last:
                        gather(t + 2, range(3 * (i - 9), min(3 * (i - 9) + 3, EARLY)))

            gather_waits(0)
            gather(0, range(F))
            tiles(pool, body)

        @block.scalar
        def _(act):
            def x_f_copy(t, a):
                wait(act, s_xt, t, XT, a + 1)
                nc.scalar.copy(x_f[:, :, 4 * a:4 * a + 4].rearrange("f b d -> f d b"),
                               misc[0:F, 0:4 * P].rearrange("f (d b) -> f d b", d=4)).then_inc(s_xf, 1)

            def z_t_copy(t, i, part):
                if part == 0:
                    wait(act, s_cin0, t, GPT, i - 1)
                    wait(act, s_zt, t, 2 * GPT, 2 * i + 1)
                    nc.scalar.copy(z_t[:, i % 2, 0:4, :], zt[:, :]).then_inc(s_ztc, 1)
                    return
                wait(act, s_zt, t, 2 * GPT, 2 * i + 2)
                nc.scalar.copy(z_t[:, i % 2, 4:6, :], zt[:, 0:2 * P]).then_inc(s_ztc, 1)
                nc.scalar.copy(z_t[0:KLAST, i % 2, 6, :], zt[0:KLAST, 2 * P:3 * P]).then_inc(s_ztc, 1)

            def x1_high(t, i):
                wait(act, s_ydve, t, GPT * HALF, HALF * (i - 1))
                wait(act, s_cin0, t, GPT, i + 1)
                nc.scalar.activation(x1_hi[:, i % 2, :], cin0, ACT.Identity,
                                     bias=b0_sb[:, 0:1]).then_inc(s_x1hi, 1)

            def g_copy(t, i):
                wait(act, s_g, t, GPT, i + 1)
                if i == 0:
                    wait(act, s_cin2, t, 1, 0)
                    wait(act, s_ztop1, t, 1, 0)
                nc.scalar.copy(g_sb[:, :, GB * i:GB * i + GB].rearrange("k j b -> k b j"),
                               g_ps[:, 0:GB * FJ].rearrange("k (b j) -> k b j", b=GB)).then_inc(s_gc, 1)

            def scale(t, i, m):
                c = 2 * m
                slot = (HALF * i + m) % SLOTS
                wait(act, s_yact, t, GPT * HALF, HALF * i + m + 1)
                q = HALF * i + m - SLOTS
                n = POOL_STEPS * (q // HALF) + max(q % HALF - 1, 0) + 1
                wait(act, s_pool, t, GPT * POOL_STEPS, n)
                for k, j in enumerate(chunk_j(c)):
                    ins = nc.scalar.activation(scaled[:, slot, k * H:(k + 1) * H],
                                               y_act[(HALF * i + m) % 2][:, k * H:(k + 1) * H], ACT.Copy,
                                               scale=x_now[:, i % 4, j:j + 1])
                ins.then_inc(s_scaled, 1)

            def res1_copy(t):
                wait(act, s_gc, t, GPT, GPT)
                wait(act, s_h1p, t, 1, 0)
                nc.scalar.copy(z_top[:, 1, :], g_sb[:, F, :]).then_inc(s_ztop1, 1)

            def res2_copy(t):
                wait(act, s_cin2, t, 1, 1)
                nc.scalar.activation(z_top[:, 2, :], misc[:, 0:P], ACT.Identity, bias=b2_16[:, 0:1]).then_inc(s_ztop2, 1)

            def relu1(t):
                wait(act, s_h1p, t, 1, 1)
                wait(act, s_h2p, t, 1, 0)
                for m in range(N1 // P):
                    ins = nc.scalar.activation(h1[:, m, :], misc[:, m * P:(m + 1) * P], ACT.Relu, bias=bt1_sb[:, m:m + 1])
                ins.then_inc(s_h1, 1)

            def relu2(t):
                wait(act, s_h2p, t, 1, 1)
                wait(act, s_yp, t, 1, 0)
                for m in range(N2 // P):
                    ins = nc.scalar.activation(h2[:, m, :], misc[:, m * P:(m + 1) * P], ACT.Relu, bias=bt2_sb[:, m:m + 1])
                ins.then_inc(s_h2, 1)

            def y_copy(t):
                wait(act, s_yp, t, 1, 1)
                wait(act, s_out, t, 16, 0)
                nc.scalar.copy(y_sb[:, :], misc[0:1, 0:P]).then_inc(s_y, 1)

            def body(t, first, last):
                for i in range(GPT):
                    wait(act, s_now, t, GPT, i + 1)
                    scale(t, i, 0)
                    scale(t, i, 1)
                    if not (last and i + 2 >= GPT):
                        z_t_copy(t, i + 2, 0)
                    scale(t, i, 2)
                    if not (last and i + 1 >= GPT):
                        x1_high(t, i + 1)
                    if not last and i in (7, 8):
                        x_f_copy(t + 1, 2 * (i - 7))
                    scale(t, i, 3)
                    if not (last and i + 2 >= GPT):
                        z_t_copy(t, i + 2, 1)
                    scale(t, i, 4)
                    if not first:
                        if i == 1:
                            res1_copy(t - 1)
                            res2_copy(t - 1)
                        if i == 2:
                            relu1(t - 1)
                        if i == 3:
                            relu2(t - 1)
                        if i == 4:
                            y_copy(t - 1)
                    if i > 0:
                        g_copy(t, i - 1)
                    elif not first:
                        g_copy(t - 1, GPT - 1)
                    if not last and i in (7, 8):
                        x_f_copy(t + 1, 2 * (i - 7) + 1)

            act.wait_ge(s_w1, 16)
            nc.scalar.copy(w1_hi[:, :], w1_raw[:, :]).then_inc(s_w1hi, 1)
            for a in range(4):
                x_f_copy(0, a)
            for i in range(2):
                for part in range(2):
                    z_t_copy(0, i, part)
            act.wait_ge(s_const, 80)
            x1_high(0, 0)
            act.wait_ge(s_top, 16 * 7)
            act.wait_ge(s_bias, 2)
            tiles(act, body)
            g_copy(TILES - 1, GPT - 1)
            res1_copy(TILES - 1)
            res2_copy(TILES - 1)
            relu1(TILES - 1)
            relu2(TILES - 1)
            y_copy(TILES - 1)

        @block.vector
        def _(dve):
            def x_bd_copy(t, half):
                wait(dve, s_xt, t, XT, 5 + half)
                g0 = half * GPT // 2
                wait(dve, s_z, t, GPT, g0 - GPT // 2)
                wait(dve, s_now, t, GPT, g0 - GPT // 2)
                src = misc[:, 0:GPT // 2 * F].rearrange("p (g f) -> p g f", f=F)
                nc.vector.tensor_copy(x_bd[:, g0:g0 + GPT // 2, 0:F], src).then_inc(s_xbd, 1)
                nc.vector.tensor_copy(x_bd[:, g0:g0 + GPT // 2, F:WRAP], src[:, :, 0:WRAP - F]).then_inc(s_xbd, 1)

            def products(t, i):
                g = i % GPT
                wait(dve, s_xbd, t, 4, 4 * (i // GPT) + (2 if g < GPT // 2 else 4))
                wait(dve, s_zt, t, 2 * GPT, 2 * (i - 1))
                a = x_bd[:, g, 0:F].unsqueeze(1).broadcast_to([P, SHIFTS, F])
                shifted = bass.AP(x_bd, g * WRAP, [[GPT * WRAP, P], [1, SHIFTS], [1, F]])
                nc.vector.tensor_tensor(z[:, i % 2, :].rearrange("p (s f) -> p s f", s=SHIFTS), a, shifted,
                                        ALU.mult).then_inc(s_z, 1)

            def x_now_copy(t, i):
                g = i % GPT
                wait(dve, s_xbd, t, 4, 4 * (i // GPT) + (2 if g < GPT // 2 else 4))
                wait(dve, s_scaled, t, GPT * HALF, HALF * (i - 3))
                wait(dve, s_steps, t, GPT * STEPS, STEPS * (i - 3))
                wait(dve, s_diag, t, GPT, i - 3)
                nc.vector.tensor_copy(x_now[:, i % 4, 0:F], x_bd[:, g, 0:F]).then_inc(s_now, 1)

            def res0_sum(t, i):
                if i % GPT == 0:
                    wait(dve, s_ztop0, t, 1, i // GPT)
                wait(dve, s_x1hi, t, GPT, i + 1)
                g = i % GPT
                nc.vector.tensor_reduce(res0[:, GB * g:GB * g + GB], cin0.rearrange("h (b d) -> h b d", d=D),
                                        AX_X, ALU.add).then_inc(s_res0, 1)

            def x1_low(t, i):
                wait(dve, s_ydve, t, GPT * HALF, HALF * (i - 1))
                wait(dve, s_x1hi, t, GPT, i + 1)
                nc.vector.scalar_tensor_tensor(out=x1_lo[:, i % 2, :], in0=cin0, scalar=b0_sb[:, 0:1],
                                               in1=x1_hi[:, i % 2, :].bitcast(F32), op0=ALU.add,
                                               op1=ALU.subtract).then_inc(s_x1lo, 1)

            def multiply_add(t, i, m):
                c = 2 * m + 1
                wait(dve, s_ydve, t, GPT * HALF, HALF * i + m + 1)
                bank = y_dve[(HALF * i + m) % 2]
                for k, j in enumerate(chunk_j(c)):
                    n = DVE_J.index(j)
                    acc = parts[:, i % 2, n % 2, :]
                    y = bank[:, k * H:(k + 1) * H]
                    x = x_now[:, i % 4, j:j + 1]
                    wait(dve, s_steps, t, GPT * STEPS, STEPS * i + n - 1)
                    if n == 0:
                        wait(dve, s_x2, t, GPT, i - 1)
                    if n == 1:
                        ins = nc.vector.tensor_scalar(acc, y, x, None, ALU.mult)
                    else:
                        ins = nc.vector.scalar_tensor_tensor(out=acc, in0=y, scalar=x,
                                                             in1=b1_rows[:, :] if n == 0 else acc,
                                                             op0=ALU.mult, op1=ALU.add)
                    ins.then_inc(s_steps, 1)

            def x2_sum(t, i):
                wait(dve, s_pool, t, GPT * POOL_STEPS, POOL_STEPS * (i + 1))
                wait(dve, s_steps, t, GPT * STEPS, STEPS * (i + 1))
                wait(dve, s_g, t, GPT, i - 1)
                nc.vector.tensor_reduce(x2[:, i % 2, :], parts[:, i % 2, :, :].rearrange("p s h -> p h s"), AX_X,
                                        ALU.add).then_inc(s_x2, 1)

            def x_diagonal(t, i):
                wait(dve, s_g, t, GPT, i - 1)
                nc.vector.tensor_tensor(x_diag[:, i % 2, :, :], mask[:, :].unsqueeze(2).broadcast_to([P, GB, FJ]),
                                        x_now[:, i % 4, :].unsqueeze(1).broadcast_to([P, GB, FJ]),
                                        ALU.mult).then_inc(s_diag, 1)

            def body(t, first, last):
                for i in range(GPT):
                    wait(dve, s_now, t, GPT, i + 1)
                    multiply_add(t, i, 0)
                    if not (last and i + 3 >= GPT):
                        products(t, i + 3)
                    multiply_add(t, i, 1)
                    if i > 0:
                        x2_sum(t, i - 1)
                    elif not first:
                        x2_sum(t - 1, GPT - 1)
                    multiply_add(t, i, 2)
                    if i == GPT - 1:
                        wait(dve, s_res0, t, GPT, GPT)
                        wait(dve, s_h1p, t, 1, 0)
                        nc.vector.tensor_scalar(z_top[:, 0, :], res0[:, :], b0_16[:, 0:1], None,
                                                ALU.add).then_inc(s_ztop0, 1)
                    if not (last and i + 1 >= GPT):
                        res0_sum(t, i + 1)
                        x1_low(t, i + 1)
                    multiply_add(t, i, 3)
                    x_diagonal(t, i)
                    multiply_add(t, i, 4)
                    if not (last and i + 3 >= GPT):
                        x_now_copy(t, i + 3)
                    if not last and i in (10, 13):
                        x_bd_copy(t + 1, 0 if i == 10 else 1)

            nc.vector.memset(x_now[:, :, F:FJ], 1.0).then_inc(s_ones, 1)
            dve.wait_ge(s_const, 80)
            nc.vector.tensor_scalar(b0_16[:, :], b0_sb[:, :], float(D), None, ALU.mult).then_inc(s_bias, 1)
            nc.vector.tensor_scalar(b2_16[:, :], b2_sb[:, :], float(D), None, ALU.mult).then_inc(s_bias, 1)
            dve.wait_ge(s_w0, 32)
            nc.vector.tensor_tensor(w0[:, :, :], w0[:, :, :], w0_other[:, :, :], ALU.add).then_inc(s_w0sum, 1)
            dve.wait_ge(s_w1hi, 1)
            nc.vector.tensor_tensor(w1_lo[:, :], w1_raw[:, :], w1_hi[:, :].bitcast(F32),
                                    ALU.subtract).then_inc(s_w1lo, 1)
            x_bd_copy(0, 0)
            x_bd_copy(0, 1)
            for i in range(3):
                products(0, i)
                x_now_copy(0, i)
            res0_sum(0, 0)
            x1_low(0, 0)
            dve.wait_ge(s_bias, 2)
            dve.wait_ge(s_ones, 1)
            tiles(dve, body)
            x2_sum(TILES - 1, GPT - 1)

        @block.tensor
        def _(pe):
            def x_one_waits(t, a):
                if a == 0:
                    wait(pe, s_gather, t, 16 * F, 16 * F)
                    wait(pe, s_y, t, 1, -1)
                    wait(pe, s_xbd, t, 4, 0)
                else:
                    wait(pe, s_xf, t, 4, a)

            def x_two_waits(t, half):
                wait(pe, s_xf, t, 4, 4)
                if half == 1:
                    wait(pe, s_xbd, t, 4, 2)

            def x_stage_one(t, a):
                for k in range(4):
                    d = 4 * a + k
                    ins = nc.tensor.transpose(misc[0:F, k * P:(k + 1) * P],
                                              emb[:, :].rearrange("p (f d) -> p f d", d=D)[:, :, d], ident[:, :])
                ins.then_inc(s_xt, 1)

            def x_stage_two(t, half):
                for k in range(GPT // 2):
                    g = half * GPT // 2 + k
                    ins = nc.tensor.transpose(misc[:, k * F:(k + 1) * F], x_f[:, GB * g:GB * g + GB, :],
                                              ident[0:F, 0:F])
                ins.then_inc(s_xt, 1)

            def z_transposes(t, i, part):
                if part == 0:
                    wait(pe, s_z, t, GPT, i + 1)
                    wait(pe, s_ztc, t, 3 * GPT, 3 * i)
                    for k in range(4):
                        ins = nc.tensor.transpose(zt[:, k * P:(k + 1) * P], z[:, i % 2, k * P:(k + 1) * P], ident[:, :])
                else:
                    wait(pe, s_ztc, t, 3 * GPT, 3 * i + 1)
                    for k in range(4, KT):
                        rows = P if k < KT - 1 else KLAST
                        ins = nc.tensor.transpose(zt[0:rows, (k - 4) * P:(k - 3) * P],
                                                  z[:, i % 2, k * P:k * P + rows], ident[:, :])
                ins.then_inc(s_zt, 1)

            def layer0(t, i, ks):
                for k in ks:
                    if k == 0:
                        wait(pe, s_ztc, t, 3 * GPT, 3 * i + 3)
                        wait(pe, s_x1lo, t, GPT, i)
                        wait(pe, s_res0, t, GPT, i)
                    rows = P if k < KT - 1 else KLAST
                    ins = nc.tensor.matmul(cin0, w0[0:rows, k, :], z_t[0:rows, i % 2, k, :],
                                           start=(k == 0), stop=(k == KT - 1))
                if KT - 1 in ks:
                    ins.then_inc(s_cin0, 1)

            def layer1_chunk(t, i, c):
                m = c // 2
                n = HALF * i + m
                if c == 0:
                    wait(pe, s_x1lo, t, GPT, i + 1)
                if c % 2 == 0:
                    bank, ready = y_act[n % 2], s_yact
                    wait(pe, s_scaled, t, GPT * HALF, n - 1)
                else:
                    bank, ready = y_dve[n % 2], s_ydve
                    q = n - 2
                    wait(pe, s_steps, t, GPT * STEPS, STEPS * (q // HALF) + min(JC * (q % HALF) + JC, STEPS))
                lo, hi = JC * c * H, min(JC * c + JC, F) * H
                for p, (x, w) in enumerate(((x1_hi, w1_hi), (x1_hi, w1_lo), (x1_lo, w1_hi))):
                    ins = nc.tensor.matmul(bank[:, 0:hi - lo], x[:, i % 2, :], w[:, lo:hi], start=(p == 0), stop=(p == 2))
                ins.then_inc(ready, 1)

            def g_matmul(t, i):
                wait(pe, s_x2, t, GPT, i + 1)
                wait(pe, s_gc, t, GPT, i)
                nc.tensor.matmul(g_ps[:, 0:GB * FJ], x2[:, i % 2, :], x_diag[:, i % 2, :, :],
                                 start=True, stop=True).then_inc(s_g, 1)

            def layer2(t, js, last=False):
                for j in js:
                    if j == 0:
                        wait(pe, s_gc, t, GPT, GPT)
                        wait(pe, s_y, t, 1, 0)
                        wait(pe, s_xbd, t, 4, 4 if last else 8)
                    ins = nc.tensor.matmul(misc[:, 0:P], w2[:, j, :], g_sb[:, j, :], start=(j == 0), stop=(j == F - 1))
                    if j == F - 1:
                        ins.then_inc(s_cin2, 1)

            def top1(t, m):
                if m == 0:
                    wait(pe, s_ztop0, t, 1, 1)
                    wait(pe, s_ztop1, t, 1, 1)
                    wait(pe, s_ztop2, t, 1, 1)
                for k in range(3):
                    nc.tensor.matmul(misc[:, m * P:(m + 1) * P], wt1_z[:, k, m * P:(m + 1) * P], z_top[:, k, :],
                                     start=(k == 0), stop=False)
                ins = nc.tensor.matmul(misc[:, m * P:(m + 1) * P], wt1_dense[:, m * P:(m + 1) * P],
                                       dense[:, bass.ds(t * P, P)], start=False, stop=True)
                if m == N1 // P - 1:
                    ins.then_inc(s_h1p, 1)

            def top2(t, m):
                wait(pe, s_h1, t, 1, 1)
                for k in range(N1 // P):
                    ins = nc.tensor.matmul(misc[:, m * P:(m + 1) * P], wt2_sb[:, k, m * P:(m + 1) * P], h1[:, k, :],
                                           start=(k == 0), stop=(k == N1 // P - 1))
                if m == N2 // P - 1:
                    ins.then_inc(s_h2p, 1)

            def top3(t):
                wait(pe, s_h2, t, 1, 1)
                for k in range(N2 // P):
                    ins = nc.tensor.matmul(misc[0:1, 0:P], wt3_sb[:, k:k + 1], h2[:, k, :],
                                           start=(k == 0), stop=(k == N2 // P - 1))
                ins.then_inc(s_yp, 1)

            def body(t, first, last):
                for i in range(GPT):
                    for c in range(CHUNKS):
                        if not last and i in (7, 8) and c in (3, 7):
                            x_one_waits(t + 1, 2 * (i - 7) + (c == 7))
                        if not last and i in (10, 13) and c == 6:
                            x_two_waits(t + 1, int(i == 13))
                        layer1_chunk(t, i, c)
                        if c in (2, 6) and not (last and i + 2 >= GPT):
                            z_transposes(t, i + 2, int(c == 6))
                        if 1 <= c <= 4 and not (last and i + 1 >= GPT):
                            layer0(t, i + 1, range(2 * c - 2, min(2 * c, KT)))
                        if c == 7:
                            if i > 0:
                                g_matmul(t, i - 1)
                            elif not first:
                                g_matmul(t - 1, GPT - 1)
                        if not first:
                            if i == 0 and c == 9:
                                layer2(t - 1, range(0, 4))
                            if i == 1 and c <= 6:
                                layer2(t - 1, range(4 + 5 * c, 9 + 5 * c))
                            if i == 2 and c in (4, 5, 6, 8):
                                top1(t - 1, (4, 5, 6, 8).index(c))
                            if i == 3 and c in (5, 6):
                                top2(t - 1, c - 5)
                            if i == 4 and c == 5:
                                top3(t - 1)
                        if not last:
                            if i in (7, 8) and c in (3, 7):
                                x_stage_one(t + 1, 2 * (i - 7) + (c == 7))
                            if i in (10, 13) and c == 6:
                                x_stage_two(t + 1, int(i == 13))

            pe.wait_ge(s_const, 80)
            for a in range(4):
                x_one_waits(0, a)
                x_stage_one(0, a)
            for half in range(2):
                x_two_waits(0, half)
                x_stage_two(0, half)
            for i in range(2):
                z_transposes(0, i, 0)
                z_transposes(0, i, 1)
            pe.wait_ge(s_w0sum, 1)
            layer0(0, 0, range(KT))
            pe.wait_ge(s_w1lo, 1)
            pe.wait_ge(s_w2, 16)
            pe.wait_ge(s_top, 16 * 7)
            tiles(pe, body)
            g_matmul(TILES - 1, GPT - 1)
            layer2(TILES - 1, range(F), last=True)
            for m in range(N1 // P):
                top1(TILES - 1, m)
            for m in range(N2 // P):
                top2(TILES - 1, m)
            top3(TILES - 1)


def kernel(**inputs):
    import numpy as np
    import concourse.bacc as bacc
    from concourse.bass_utils import run_bass_kernel_spmd

    nc = bacc.Bacc("TRN2", target_bir_lowering=False, num_devices=1)
    a = {k: np.asarray(v) for k, v in inputs.items()}

    w0 = np.concatenate([a["L0_rec_W0"], np.zeros((H, 1), np.float32)], axis=1)
    zero = F * F
    i1 = np.tile(np.arange(F), SHIFTS)
    i2 = (i1 + np.repeat(np.arange(SHIFTS), F)) % F
    order_a, order_b = np.full(KT * P, zero), np.full(KT * P, zero)
    order_a[:PAIRS] = i1 * F + i2
    order_b[:PAIRS] = np.where(i1 == i2, zero, i2 * F + i1)

    def pair_rows(order):
        return np.ascontiguousarray(w0[:, order].T.reshape(KT, P, H).transpose(1, 0, 2))

    def by_k(w):
        return w.reshape(H, F, H).transpose(2, 1, 0)

    arrays = {f"tbl_{f}": a[f"tbl_{f}"] for f in range(F)}
    arrays |= {
        "ids": np.concatenate([a["ids"], a["ids"][:P]]),
        "dense_t": a["dense_ctx"].T,
        "w0a": pair_rows(order_a), "w0b": pair_rows(order_b), "b0": a["L0_rec_b0"].reshape(H, 1),
        "w1_t": by_k(a["L0_rec_W1"]).reshape(H, F * H), "b1": a["L0_rec_b1"],
        "w2_t": by_k(a["L0_rec_W2"]), "b2": a["L0_rec_b2"].reshape(H, 1),
        "wt1": a["W_top1"], "bt1": a["b_top1"].reshape(N1 // P, P).T,
        "wt2": a["W_top2"], "bt2": a["b_top2"].reshape(N2 // P, P).T,
        "wt3": a["W_top3"].reshape(N2 // P, P).T,
        "identity": np.eye(P, dtype=np.float32),
        "row_mask": np.repeat(np.eye(GB, dtype=np.float32), D, axis=0),
    }
    arrays = {f"in_{k}": np.ascontiguousarray(v) for k, v in arrays.items()}
    args = [nc.dram_tensor(k, v.shape, mybir.dt.from_np(v.dtype), kind="ExternalInput").ap() for k, v in arrays.items()]
    out = nc.dram_tensor("out_y", (1, B), F32, kind="ExternalOutput").ap()
    dlrm_cin_kernel(nc, args[:F], *args[F:], out)
    r = run_bass_kernel_spmd(nc, [arrays], core_ids=[0])
    return r.results[0]["out_y"].reshape(B, 1)
```

```python
from contextlib import ExitStack

import concourse.bass as bass
from concourse import mybir

P = 128
B, F, D, H = 1024, 39, 16, 128
TILES = B // P
GB = P // D
GPT = P // GB
SHIFTS = (F + 1) // 2
WRAP = F + SHIFTS - 1
SPK = P // F
KR = SPK * F
KT = -(-SHIFTS // SPK)
KLAST = (SHIFTS - (KT - 1) * SPK) * F
QG = 4
QUARTERS = GPT // QG
QC = QG * P
LAYOUTS = SHIFTS + SPK
NDENSE, N1, N2 = 16, 512, 256
FJ = F + 1
JC = 4
CHUNKS = -(-F // JC)
HALF = CHUNKS // 2
SLOTS = 8
DVE_J = [j for c in range(1, CHUNKS, 2) for j in range(JC * c, min(JC * c + JC, F))]
STEPS = len(DVE_J)
POOL_STEPS = HALF
EARLY = 15
XT = 6

F32 = mybir.dt.float32
F32R = mybir.dt.float32r
I32 = mybir.dt.int32
ALU = mybir.AluOpType
ACT = mybir.ActivationFunctionType
AX_X = mybir.AxisListType.X


def wait(eng, sem, t, per_tile, n):
    if isinstance(t, int) and t * per_tile + n <= 0:
        return
    eng.wait_ge(sem, t * per_tile + n)


def chunk_j(c):
    return range(JC * c, min(JC * c + JC, F))


def dlrm_cin_kernel(nc, tables, ids, dense_t, w0a, w0b, b0, w1_t, b1, w2_t, b2,
                    wt1, bt1, wt2, bt2, wt3, identity, row_mask, out):
    ctx = ExitStack()
    with ctx:
        def sb(name, shape, dt=F32):
            return ctx.enter_context(nc.sbuf_tensor(name, shape, dt))

        def pb(name):
            return ctx.enter_context(nc.psum_tensor(name, [P, 512], F32))

        def sem(name):
            return ctx.enter_context(nc.semaphore(name))

        w1_hi = sb("w1_hi", [P, F * H], F32R)
        w1_lo = sb("w1_lo", [P, F * H], F32R)
        w2 = sb("w2", [P, F, H])
        w0 = sb("w0", [KR, KT, H])
        w0_other = sb("w0_other", [KR, KT, H])
        wt1_z = sb("wt1_z", [P, 3, N1])
        wt1_dense = sb("wt1_dense", [NDENSE, N1])
        wt2_sb = sb("wt2_sb", [P, N1 // P, N2])
        wt3_sb = sb("wt3_sb", [P, N2 // P])
        bt1_sb = sb("bt1_sb", [P, N1 // P])
        bt2_sb = sb("bt2_sb", [P, N2 // P])
        b0_sb = sb("b0_sb", [P, 1])
        b0_16 = sb("b0_16", [P, 1])
        b1_rows = sb("b1_rows", [P, H])
        b2_sb = sb("b2_sb", [P, 1])
        b2_16 = sb("b2_16", [P, 1])
        ident = sb("ident", [P, P])
        mask = sb("mask", [P, GB])
        dense = sb("dense", [NDENSE, B])
        ids_tile = sb("ids_tile", [P, F], I32)
        emb = sb("emb", [P, WRAP * D])
        x_f = sb("x_f", [WRAP, P, D])
        x_bd = sb("x_bd", [P, GPT, F])
        x_now = sb("x_now", [P, 4, FJ])
        x_same = sb("x_same", [P, 2, QC])
        x_shift = sb("x_shift", [P, 2, KT, QC])
        z = sb("z", [P, 2, KT, P])
        x1_hi = sb("x1_hi", [P, 2, P], F32R)
        x1_lo = sb("x1_lo", [P, 2, P], F32R)
        scaled = sb("scaled", [P, SLOTS, JC * H])
        pool_sum = sb("pool_sum", [P, JC * H])
        parts = sb("parts", [P, 2, 4, H])
        x2 = sb("x2", [P, 2, H])
        x_diag = sb("x_diag", [P, 2, GB, FJ])
        g_sb = sb("g_sb", [P, FJ, P])
        w1_raw = g_sb[:, 0:F, :].rearrange("k j h -> k (j h)")
        res0 = sb("res0", [P, P])
        z_top = sb("z_top", [P, 3, P])
        h1 = sb("h1", [P, N1 // P, P])
        h2 = sb("h2", [P, N2 // P, P])
        y_sb = sb("y_sb", [1, P])

        y_act = [pb("y_act0"), pb("y_act1")]
        y_dve = [pb("y_dve0"), pb("y_dve1")]
        cin0 = pb("cin0")[:, 0:P]
        g_ps = pb("g_ps")
        misc = pb("misc")

        s_ids = sem("ids_loaded")
        s_gather = sem("gathered")
        s_w1 = sem("w1_loaded")
        s_w0 = sem("w0_loaded")
        s_w2 = sem("w2_loaded")
        s_const = sem("consts_loaded")
        s_top = sem("top_loaded")
        s_ones = sem("ones_set")
        s_w1hi = sem("w1_hi_made")
        s_w1lo = sem("w1_lo_made")
        s_w0sum = sem("w0_summed")
        s_bias = sem("biases_made")
        s_xt = sem("x_transposed")
        s_xf = sem("x_f_written")
        s_xbd = sem("x_bd_written")
        s_z = sem("z_made")
        s_now = sem("x_now_made")
        s_wrap = sem("emb_wrapped")
        s_lay = [sem("x_laid_out_even"), sem("x_laid_out_odd")]
        s_cin0 = sem("cin0_summed")
        s_x1hi = sem("x1_hi_made")
        s_x1lo = sem("x1_lo_made")
        s_res0 = sem("res0_made")
        s_yact = sem("y_for_act")
        s_ydve = sem("y_for_dve")
        s_scaled = sem("scaled")
        s_steps = sem("dve_steps")
        s_pool = sem("pool_steps")
        s_x2 = sem("x2_made")
        s_diag = sem("x_diag_made")
        s_g = sem("g_summed")
        s_gc = sem("g_written")
        s_cin2 = sem("cin2_summed")
        s_ztop0 = sem("z_top0_made")
        s_ztop1 = sem("z_top1_made")
        s_ztop2 = sem("z_top2_made")
        s_h1p = sem("h1_summed")
        s_h1 = sem("h1_made")
        s_h2p = sem("h2_summed")
        s_h2 = sem("h2_made")
        s_yp = sem("y_summed")
        s_y = sem("y_made")
        s_out = sem("y_stored")

        block = ctx.enter_context(nc.Block())

        def tiles(eng, body):
            body(0, True, False)
            with eng.Fori(1, TILES - 1) as t:
                body(t, False, False)
            body(TILES - 1, False, True)

        @block.sync
        def _(sp):
            def load_ids(t, row=None):
                wait(sp, s_gather, t, 16 * F, 0)
                sp.dma_start(ids_tile[:, :], ids[bass.ds(t * P if row is None else row, P), :]).then_inc(s_ids, 16)

            load_ids(0)
            sp.dma_start(ident[:, :], identity).then_inc(s_const, 16)
            sp.dma_start(mask[:, :], row_mask).then_inc(s_const, 16)
            sp.dma_start(b0_sb[:, :], b0).then_inc(s_const, 16)
            sp.dma_start(b2_sb[:, :], b2).then_inc(s_const, 16)
            sp.dma_start(b1_rows[:, :], bass.AP(b1.tensor, 0, [[0, P], [1, H]])).then_inc(s_const, 16)
            sp.dma_start(w0[:, :, :], w0a).then_inc(s_w0, 16)
            sp.dma_start(w0_other[:, :, :], w0b).then_inc(s_w0, 16)
            sp.dma_start(w1_raw, w1_t).then_inc(s_w1, 16)
            sp.dma_start(w2[:, :, :], w2_t).then_inc(s_w2, 16)
            sp.dma_start(wt1_z[:, :, :], wt1[0:3 * H, :].rearrange("(l p) n -> p l n", p=P)).then_inc(s_top, 16)
            sp.dma_start(wt1_dense[:, :], wt1[3 * H:3 * H + NDENSE, :]).then_inc(s_top, 16)
            sp.dma_start(wt2_sb[:, :, :], wt2.rearrange("(l p) n -> p l n", p=P)).then_inc(s_top, 16)
            sp.dma_start(wt3_sb[:, :], wt3).then_inc(s_top, 16)
            sp.dma_start(bt1_sb[:, :], bt1).then_inc(s_top, 16)
            sp.dma_start(bt2_sb[:, :], bt2).then_inc(s_top, 16)
            sp.dma_start(dense[:, :], dense_t).then_inc(s_top, 16)

            def lay_out(t, q):
                wait(sp, s_z, t, GPT, QG * (q - 1))
                if q == 0:
                    wait(sp, s_xf, t, 4, 4)
                cols = x_f[:, :, :].rearrange("f b d -> f (b d)")[:, q * QC:(q + 1) * QC]
                for k in range(SPK):
                    sp.dma_start(x_same[k * F:(k + 1) * F, q % 2, :], cols[0:F, :]).then_inc(s_lay[q % 2], 16)
                for s in range(SHIFTS):
                    row = s % SPK * F
                    sp.dma_start(x_shift[row:row + F, q % 2, s // SPK, :], cols[s:s + F, :]).then_inc(s_lay[q % 2], 16)

            def store(t, row=None):
                wait(sp, s_y, t, 1, 1)
                sp.dma_start(out[:, bass.ds(t * P if row is None else row, P)], y_sb[:, :]).then_inc(s_out, 16)

            def body(t, first, last):
                ids_row = out_row = None
                if not first and not last:
                    ids_row, out_row = sp.snap((t + 2) * P), sp.snap((t - 1) * P)
                lay_out(t, 2)
                if not first:
                    store(t - 1, out_row)
                lay_out(t, 3)
                if not last:
                    load_ids(t + 2, ids_row)
                    lay_out(t + 1, 0)
                    lay_out(t + 1, 1)

            load_ids(1)
            sp.wait_ge(s_ones, 2)
            lay_out(0, 0)
            lay_out(0, 1)
            tiles(sp, body)
            store(TILES - 1)
            sp.wait_ge(s_out, 16 * TILES)

        @block.gpsimd
        def _(pool):
            def gather(t, fields):
                for f in fields:
                    nc.gpsimd.indirect_dma_start(
                        out=emb[:, f * D:(f + 1) * D], out_offset=None, in_=tables[f],
                        in_offset=bass.IndirectOffsetOnAxis(ap=ids_tile[:, f:f + 1], axis=0),
                    ).then_inc(s_gather, 16)

            def gather_waits(t):
                wait(pool, s_ids, t, 16, 16)
                wait(pool, s_xt, t, XT, -2)

            def add(t, n, out_, a, b):
                wait(pool, s_pool, t, GPT * POOL_STEPS, n)
                nc.gpsimd.tensor_tensor(out_, a, b, ALU.add).then_inc(s_pool, 1)

            def body(t, first, last):
                for i in range(GPT):
                    n = POOL_STEPS * i
                    for m in range(1, HALF):
                        wait(pool, s_scaled, t, GPT * HALF, HALF * i + m + 1)
                        slot = (HALF * i + m) % SLOTS
                        add(t, n + m - 1, pool_sum[:, :], scaled[:, (slot - 1) % SLOTS, :] if m == 1 else pool_sum[:, :],
                            scaled[:, slot, :])
                    if (i == 0 and first) or (i == 11 and not last):
                        gather_waits(t + 1 if i == 0 else t + 2)
                    wait(pool, s_x2, t, GPT, i - 1)
                    add(t, n + HALF - 1, parts[:, i % 2, 2:4, :], pool_sum[:, 0:2 * H], pool_sum[:, 2 * H:4 * H])
                    if first:
                        gather(t + 1, range(5 * i, min(5 * i + 5, F)))
                    elif not last:
                        gather(t + 1, range(EARLY + 3 * i, min(EARLY + 3 * i + 3, F)))
                    if i >= 11 and not last:
                        gather(t + 2, range(3 * (i - 11), min(3 * (i - 11) + 3, EARLY)))

            gather_waits(0)
            gather(0, range(F))
            tiles(pool, body)

        @block.scalar
        def _(act):
            def x_f_copy(t, a):
                wait(act, s_xt, t, XT, a + 1)
                if a == 0:
                    for odd in range(2):
                        wait(act, s_lay[odd], t, 16 * LAYOUTS * QUARTERS // 2, 0)
                nc.scalar.copy(x_f[:, :, 4 * a:4 * a + 4].rearrange("f b d -> f d b"),
                               misc[0:WRAP, 0:4 * P].rearrange("f (d b) -> f d b", d=4)).then_inc(s_xf, 1)

            def x1_high(t, i):
                wait(act, s_ydve, t, GPT * HALF, HALF * (i - 1))
                wait(act, s_cin0, t, GPT, i + 1)
                nc.scalar.activation(x1_hi[:, i % 2, :], cin0, ACT.Identity,
                                     bias=b0_sb[:, 0:1]).then_inc(s_x1hi, 1)

            def g_copy(t, i):
                wait(act, s_g, t, GPT, i + 1)
                if i == 0:
                    wait(act, s_cin2, t, 1, 0)
                    wait(act, s_ztop1, t, 1, 0)
                nc.scalar.copy(g_sb[:, :, GB * i:GB * i + GB].rearrange("k j b -> k b j"),
                               g_ps[:, 0:GB * FJ].rearrange("k (b j) -> k b j", b=GB)).then_inc(s_gc, 1)

            def scale(t, i, m):
                c = 2 * m
                slot = (HALF * i + m) % SLOTS
                wait(act, s_yact, t, GPT * HALF, HALF * i + m + 1)
                q = HALF * i + m - SLOTS
                n = POOL_STEPS * (q // HALF) + max(q % HALF - 1, 0) + 1
                wait(act, s_pool, t, GPT * POOL_STEPS, n)
                for k, j in enumerate(chunk_j(c)):
                    ins = nc.scalar.activation(scaled[:, slot, k * H:(k + 1) * H],
                                               y_act[(HALF * i + m) % 2][:, k * H:(k + 1) * H], ACT.Copy,
                                               scale=x_now[:, i % 4, j:j + 1])
                ins.then_inc(s_scaled, 1)

            def res1_copy(t):
                wait(act, s_gc, t, GPT, GPT)
                wait(act, s_h1p, t, 1, 0)
                nc.scalar.copy(z_top[:, 1, :], g_sb[:, F, :]).then_inc(s_ztop1, 1)

            def res2_copy(t):
                wait(act, s_cin2, t, 1, 1)
                nc.scalar.activation(z_top[:, 2, :], misc[:, 0:P], ACT.Identity, bias=b2_16[:, 0:1]).then_inc(s_ztop2, 1)

            def relu1(t):
                wait(act, s_h1p, t, 1, 1)
                wait(act, s_h2p, t, 1, 0)
                for m in range(N1 // P):
                    ins = nc.scalar.activation(h1[:, m, :], misc[:, m * P:(m + 1) * P], ACT.Relu, bias=bt1_sb[:, m:m + 1])
                ins.then_inc(s_h1, 1)

            def relu2(t):
                wait(act, s_h2p, t, 1, 1)
                wait(act, s_yp, t, 1, 0)
                for m in range(N2 // P):
                    ins = nc.scalar.activation(h2[:, m, :], misc[:, m * P:(m + 1) * P], ACT.Relu, bias=bt2_sb[:, m:m + 1])
                ins.then_inc(s_h2, 1)

            def y_copy(t):
                wait(act, s_yp, t, 1, 1)
                wait(act, s_out, t, 16, 0)
                nc.scalar.copy(y_sb[:, :], misc[0:1, 0:P]).then_inc(s_y, 1)

            def body(t, first, last):
                for i in range(GPT):
                    wait(act, s_now, t, GPT, i + 1)
                    scale(t, i, 0)
                    scale(t, i, 1)
                    scale(t, i, 2)
                    if not (last and i + 1 >= GPT):
                        x1_high(t, i + 1)
                    if not last and i in (9, 10):
                        x_f_copy(t + 1, 2 * (i - 9))
                    scale(t, i, 3)
                    scale(t, i, 4)
                    if not first:
                        if i == 1:
                            res1_copy(t - 1)
                            res2_copy(t - 1)
                        if i == 2:
                            relu1(t - 1)
                        if i == 3:
                            relu2(t - 1)
                        if i == 4:
                            y_copy(t - 1)
                    if i > 0:
                        g_copy(t, i - 1)
                    elif not first:
                        g_copy(t - 1, GPT - 1)
                    if not last and i in (9, 10):
                        x_f_copy(t + 1, 2 * (i - 9) + 1)

            act.wait_ge(s_w1, 16)
            nc.scalar.copy(w1_hi[:, :], w1_raw).then_inc(s_w1hi, 1)
            for a in range(4):
                x_f_copy(0, a)
            act.wait_ge(s_const, 80)
            x1_high(0, 0)
            act.wait_ge(s_top, 16 * 7)
            act.wait_ge(s_bias, 2)
            act.wait_ge(s_w1lo, 1)
            tiles(act, body)
            g_copy(TILES - 1, GPT - 1)
            res1_copy(TILES - 1)
            res2_copy(TILES - 1)
            relu1(TILES - 1)
            relu2(TILES - 1)
            y_copy(TILES - 1)

        @block.vector
        def _(dve):
            def x_bd_copy(t, half):
                wait(dve, s_xt, t, XT, 5 + half)
                g0 = half * GPT // 2
                wait(dve, s_now, t, GPT, g0 - GPT // 2)
                src = misc[:, 0:GPT // 2 * F].rearrange("p (g f) -> p g f", f=F)
                nc.vector.tensor_copy(x_bd[:, g0:g0 + GPT // 2, :], src).then_inc(s_xbd, 1)

            def wrap(t):
                wait(dve, s_gather, t, 16 * F, 16 * F)
                wait(dve, s_xt, t, XT, -2)
                nc.vector.tensor_copy(emb[:, F * D:WRAP * D], emb[:, 0:(WRAP - F) * D]).then_inc(s_wrap, 1)

            def products(t, i):
                q = i // QG
                wait(dve, s_lay[q % 2], t, 16 * LAYOUTS * QUARTERS // 2, 16 * LAYOUTS * (q // 2 + 1))
                wait(dve, s_cin0, t, GPT, i - 1)
                cols = slice(i % QG * P, (i % QG + 1) * P)
                nc.vector.tensor_tensor(z[0:KR, i % 2, :, :],
                                        x_same[0:KR, q % 2, cols].unsqueeze(1).broadcast_to([KR, KT, P]),
                                        x_shift[0:KR, q % 2, :, cols], ALU.mult).then_inc(s_z, 1)

            def x_now_copy(t, i):
                g = i % GPT
                wait(dve, s_xbd, t, 2, 2 * (i // GPT) + (1 if g < GPT // 2 else 2))
                wait(dve, s_scaled, t, GPT * HALF, HALF * (i - 3))
                wait(dve, s_steps, t, GPT * STEPS, STEPS * (i - 3))
                wait(dve, s_diag, t, GPT, i - 3)
                nc.vector.tensor_copy(x_now[:, i % 4, 0:F], x_bd[:, g, 0:F]).then_inc(s_now, 1)

            def res0_sum(t, i):
                if i % GPT == 0:
                    wait(dve, s_ztop0, t, 1, i // GPT)
                wait(dve, s_x1hi, t, GPT, i + 1)
                g = i % GPT
                nc.vector.tensor_reduce(res0[:, GB * g:GB * g + GB], cin0.rearrange("h (b d) -> h b d", d=D),
                                        AX_X, ALU.add).then_inc(s_res0, 1)

            def x1_low(t, i):
                wait(dve, s_ydve, t, GPT * HALF, HALF * (i - 1))
                wait(dve, s_x1hi, t, GPT, i + 1)
                nc.vector.scalar_tensor_tensor(out=x1_lo[:, i % 2, :], in0=cin0, scalar=b0_sb[:, 0:1],
                                               in1=x1_hi[:, i % 2, :].bitcast(F32), op0=ALU.add,
                                               op1=ALU.subtract).then_inc(s_x1lo, 1)

            def multiply_add(t, i, m):
                c = 2 * m + 1
                wait(dve, s_ydve, t, GPT * HALF, HALF * i + m + 1)
                bank = y_dve[(HALF * i + m) % 2]
                for k, j in enumerate(chunk_j(c)):
                    n = DVE_J.index(j)
                    acc = parts[:, i % 2, n % 2, :]
                    y = bank[:, k * H:(k + 1) * H]
                    x = x_now[:, i % 4, j:j + 1]
                    wait(dve, s_steps, t, GPT * STEPS, STEPS * i + n - 1)
                    if n == 0:
                        wait(dve, s_x2, t, GPT, i - 1)
                    if n == 1:
                        ins = nc.vector.tensor_scalar(acc, y, x, None, ALU.mult)
                    else:
                        ins = nc.vector.scalar_tensor_tensor(out=acc, in0=y, scalar=x,
                                                             in1=b1_rows[:, :] if n == 0 else acc,
                                                             op0=ALU.mult, op1=ALU.add)
                    ins.then_inc(s_steps, 1)

            def x2_sum(t, i):
                wait(dve, s_pool, t, GPT * POOL_STEPS, POOL_STEPS * (i + 1))
                wait(dve, s_steps, t, GPT * STEPS, STEPS * (i + 1))
                wait(dve, s_g, t, GPT, i - 1)
                nc.vector.tensor_reduce(x2[:, i % 2, :], parts[:, i % 2, :, :].rearrange("p s h -> p h s"), AX_X,
                                        ALU.add).then_inc(s_x2, 1)

            def x_diagonal(t, i):
                wait(dve, s_g, t, GPT, i - 1)
                nc.vector.tensor_tensor(x_diag[:, i % 2, :, :], mask[:, :].unsqueeze(2).broadcast_to([P, GB, FJ]),
                                        x_now[:, i % 4, :].unsqueeze(1).broadcast_to([P, GB, FJ]),
                                        ALU.mult).then_inc(s_diag, 1)

            def body(t, first, last):
                for i in range(GPT):
                    wait(dve, s_now, t, GPT, i + 1)
                    multiply_add(t, i, 0)
                    if not (last and i + 2 >= GPT):
                        products(t, i + 2)
                    multiply_add(t, i, 1)
                    if i > 0:
                        x2_sum(t, i - 1)
                    elif not first:
                        x2_sum(t - 1, GPT - 1)
                    multiply_add(t, i, 2)
                    if i == GPT - 1:
                        wait(dve, s_res0, t, GPT, GPT)
                        wait(dve, s_h1p, t, 1, 0)
                        nc.vector.tensor_scalar(z_top[:, 0, :], res0[:, :], b0_16[:, 0:1], None,
                                                ALU.add).then_inc(s_ztop0, 1)
                    if not (last and i + 1 >= GPT):
                        res0_sum(t, i + 1)
                        x1_low(t, i + 1)
                    multiply_add(t, i, 3)
                    x_diagonal(t, i)
                    multiply_add(t, i, 4)
                    if not (last and i + 3 >= GPT):
                        x_now_copy(t, i + 3)
                    if not last and i in (11, 13):
                        x_bd_copy(t + 1, int(i == 13))
                    if not last and i == 8:
                        wrap(t + 1)

            nc.vector.memset(x_now[:, :, F:FJ], 1.0).then_inc(s_ones, 1)
            nc.vector.memset(x_shift[:, :, KT - 1, :], 0.0).then_inc(s_ones, 1)
            dve.wait_ge(s_const, 80)
            nc.vector.tensor_scalar(b0_16[:, :], b0_sb[:, :], float(D), None, ALU.mult).then_inc(s_bias, 1)
            nc.vector.tensor_scalar(b2_16[:, :], b2_sb[:, :], float(D), None, ALU.mult).then_inc(s_bias, 1)
            dve.wait_ge(s_w0, 32)
            nc.vector.tensor_tensor(w0[:, :, :], w0[:, :, :], w0_other[:, :, :], ALU.add).then_inc(s_w0sum, 1)
            dve.wait_ge(s_w1hi, 1)
            nc.vector.tensor_tensor(w1_lo[:, :], w1_raw, w1_hi[:, :].bitcast(F32),
                                    ALU.subtract).then_inc(s_w1lo, 1)
            wrap(0)
            x_bd_copy(0, 0)
            x_bd_copy(0, 1)
            for i in range(2):
                products(0, i)
            for i in range(3):
                x_now_copy(0, i)
            res0_sum(0, 0)
            x1_low(0, 0)
            dve.wait_ge(s_bias, 2)
            dve.wait_ge(s_ones, 2)
            tiles(dve, body)
            x2_sum(TILES - 1, GPT - 1)

        @block.tensor
        def _(pe):
            def x_one_waits(t, a):
                if a == 0:
                    wait(pe, s_gather, t, 16 * F, 16 * F)
                    wait(pe, s_wrap, t, 1, 1)
                    wait(pe, s_y, t, 1, -1)
                    wait(pe, s_xbd, t, 2, 0)
                else:
                    wait(pe, s_xf, t, 4, a)

            def x_two_waits(t, half):
                wait(pe, s_xf, t, 4, 4)
                if half == 1:
                    wait(pe, s_xbd, t, 2, 1)

            def x_stage_one(t, a):
                for k in range(4):
                    d = 4 * a + k
                    ins = nc.tensor.transpose(misc[0:WRAP, k * P:(k + 1) * P],
                                              emb[:, :].rearrange("p (f d) -> p f d", d=D)[:, :, d], ident[:, :])
                ins.then_inc(s_xt, 1)

            def x_stage_two(t, half):
                for k in range(GPT // 2):
                    g = half * GPT // 2 + k
                    ins = nc.tensor.transpose(misc[:, k * F:(k + 1) * F], x_f[0:F, GB * g:GB * g + GB, :],
                                              ident[0:F, 0:F])
                ins.then_inc(s_xt, 1)

            def layer0(t, i, ks):
                for k in ks:
                    if k == 0:
                        wait(pe, s_z, t, GPT, i + 1)
                        wait(pe, s_x1lo, t, GPT, i)
                        wait(pe, s_res0, t, GPT, i)
                    rows = KR if k < KT - 1 else KLAST
                    ins = nc.tensor.matmul(cin0, w0[0:rows, k, :], z[0:rows, i % 2, k, :],
                                           start=(k == 0), stop=(k == KT - 1))
                if KT - 1 in ks:
                    ins.then_inc(s_cin0, 1)

            def layer1_chunk(t, i, c):
                m = c // 2
                n = HALF * i + m
                if c == 0:
                    wait(pe, s_x1lo, t, GPT, i + 1)
                if c % 2 == 0:
                    bank, ready = y_act[n % 2], s_yact
                    wait(pe, s_scaled, t, GPT * HALF, n - 1)
                else:
                    bank, ready = y_dve[n % 2], s_ydve
                    q = n - 2
                    wait(pe, s_steps, t, GPT * STEPS, STEPS * (q // HALF) + min(JC * (q % HALF) + JC, STEPS))
                lo, hi = JC * c * H, min(JC * c + JC, F) * H
                for p, (x, w) in enumerate(((x1_hi, w1_hi), (x1_hi, w1_lo), (x1_lo, w1_hi))):
                    ins = nc.tensor.matmul(bank[:, 0:hi - lo], x[:, i % 2, :], w[:, lo:hi], start=(p == 0), stop=(p == 2))
                ins.then_inc(ready, 1)

            def g_matmul(t, i):
                wait(pe, s_x2, t, GPT, i + 1)
                wait(pe, s_gc, t, GPT, i)
                nc.tensor.matmul(g_ps[:, 0:GB * FJ], x2[:, i % 2, :], x_diag[:, i % 2, :, :],
                                 start=True, stop=True).then_inc(s_g, 1)

            def layer2(t, js, last=False):
                for j in js:
                    if j == 0:
                        wait(pe, s_gc, t, GPT, GPT)
                        wait(pe, s_y, t, 1, 0)
                        wait(pe, s_xbd, t, 2, 2 if last else 4)
                    ins = nc.tensor.matmul(misc[:, 0:P], w2[:, j, :], g_sb[:, j, :], start=(j == 0), stop=(j == F - 1))
                    if j == F - 1:
                        ins.then_inc(s_cin2, 1)

            def top1(t, m):
                if m == 0:
                    wait(pe, s_ztop0, t, 1, 1)
                    wait(pe, s_ztop1, t, 1, 1)
                    wait(pe, s_ztop2, t, 1, 1)
                for k in range(3):
                    nc.tensor.matmul(misc[:, m * P:(m + 1) * P], wt1_z[:, k, m * P:(m + 1) * P], z_top[:, k, :],
                                     start=(k == 0), stop=False)
                ins = nc.tensor.matmul(misc[:, m * P:(m + 1) * P], wt1_dense[:, m * P:(m + 1) * P],
                                       dense[:, bass.ds(t * P, P)], start=False, stop=True)
                if m == N1 // P - 1:
                    ins.then_inc(s_h1p, 1)

            def top2(t, m):
                wait(pe, s_h1, t, 1, 1)
                for k in range(N1 // P):
                    ins = nc.tensor.matmul(misc[:, m * P:(m + 1) * P], wt2_sb[:, k, m * P:(m + 1) * P], h1[:, k, :],
                                           start=(k == 0), stop=(k == N1 // P - 1))
                if m == N2 // P - 1:
                    ins.then_inc(s_h2p, 1)

            def top3(t):
                wait(pe, s_h2, t, 1, 1)
                for k in range(N2 // P):
                    ins = nc.tensor.matmul(misc[0:1, 0:P], wt3_sb[:, k:k + 1], h2[:, k, :],
                                           start=(k == 0), stop=(k == N2 // P - 1))
                ins.then_inc(s_yp, 1)

            def body(t, first, last):
                for i in range(GPT):
                    for c in range(CHUNKS):
                        if not last and i in (9, 10) and c in (3, 7):
                            x_one_waits(t + 1, 2 * (i - 9) + (c == 7))
                        if not last and i in (11, 13) and c == 6:
                            x_two_waits(t + 1, int(i == 13))
                        layer1_chunk(t, i, c)
                        if 1 <= c <= 4 and not (last and i + 1 >= GPT):
                            layer0(t, i + 1, range(2 * c - 2, min(2 * c, KT)))
                        if c == 7:
                            if i > 0:
                                g_matmul(t, i - 1)
                            elif not first:
                                g_matmul(t - 1, GPT - 1)
                        if not first:
                            if i == 0 and c == 9:
                                layer2(t - 1, range(0, 4))
                            if i == 1 and c <= 6:
                                layer2(t - 1, range(4 + 5 * c, 9 + 5 * c))
                            if i == 2 and c in (4, 5, 6, 8):
                                top1(t - 1, (4, 5, 6, 8).index(c))
                            if i == 3 and c in (5, 6):
                                top2(t - 1, c - 5)
                            if i == 4 and c == 5:
                                top3(t - 1)
                        if not last:
                            if i in (9, 10) and c in (3, 7):
                                x_stage_one(t + 1, 2 * (i - 9) + (c == 7))
                            if i in (11, 13) and c == 6:
                                x_stage_two(t + 1, int(i == 13))

            pe.wait_ge(s_const, 80)
            for a in range(4):
                x_one_waits(0, a)
                x_stage_one(0, a)
            for half in range(2):
                x_two_waits(0, half)
                x_stage_two(0, half)
            pe.wait_ge(s_w0sum, 1)
            layer0(0, 0, range(KT))
            pe.wait_ge(s_w1lo, 1)
            pe.wait_ge(s_w2, 16)
            pe.wait_ge(s_top, 16 * 7)
            tiles(pe, body)
            g_matmul(TILES - 1, GPT - 1)
            layer2(TILES - 1, range(F), last=True)
            for m in range(N1 // P):
                top1(TILES - 1, m)
            for m in range(N2 // P):
                top2(TILES - 1, m)
            top3(TILES - 1)


def kernel(**inputs):
    import numpy as np
    import concourse.bacc as bacc
    from concourse.bass_utils import run_bass_kernel_spmd

    nc = bacc.Bacc("TRN2", target_bir_lowering=False, num_devices=1)
    a = {k: np.asarray(v) for k, v in inputs.items()}

    w0 = np.concatenate([a["L0_rec_W0"], np.zeros((H, 1), np.float32)], axis=1)
    zero = F * F
    i1 = np.tile(np.arange(F), SHIFTS)
    i2 = (i1 + np.repeat(np.arange(SHIFTS), F)) % F
    order_a, order_b = np.full(KT * KR, zero), np.full(KT * KR, zero)
    order_a[:len(i1)] = i1 * F + i2
    order_b[:len(i1)] = np.where(i1 == i2, zero, i2 * F + i1)

    def pair_rows(order):
        return np.ascontiguousarray(w0[:, order].T.reshape(KT, KR, H).transpose(1, 0, 2))

    def by_k(w):
        return w.reshape(H, F, H).transpose(2, 1, 0)

    arrays = {f"tbl_{f}": a[f"tbl_{f}"] for f in range(F)}
    arrays |= {
        "ids": np.concatenate([a["ids"], a["ids"][:P]]),
        "dense_t": a["dense_ctx"].T,
        "w0a": pair_rows(order_a), "w0b": pair_rows(order_b), "b0": a["L0_rec_b0"].reshape(H, 1),
        "w1_t": by_k(a["L0_rec_W1"]).reshape(H, F * H), "b1": a["L0_rec_b1"],
        "w2_t": by_k(a["L0_rec_W2"]), "b2": a["L0_rec_b2"].reshape(H, 1),
        "wt1": a["W_top1"], "bt1": a["b_top1"].reshape(N1 // P, P).T,
        "wt2": a["W_top2"], "bt2": a["b_top2"].reshape(N2 // P, P).T,
        "wt3": a["W_top3"].reshape(N2 // P, P).T,
        "identity": np.eye(P, dtype=np.float32),
        "row_mask": np.repeat(np.eye(GB, dtype=np.float32), D, axis=0),
    }
    arrays = {f"in_{k}": np.ascontiguousarray(v) for k, v in arrays.items()}
    args = [nc.dram_tensor(k, v.shape, mybir.dt.from_np(v.dtype), kind="ExternalInput").ap() for k, v in arrays.items()]
    out = nc.dram_tensor("out_y", (1, B), F32, kind="ExternalOutput").ap()
    dlrm_cin_kernel(nc, args[:F], *args[F:], out)
    r = run_bass_kernel_spmd(nc, [arrays], core_ids=[0])
    return r.results[0]["out_y"].reshape(B, 1)
```

```python
from contextlib import ExitStack

import concourse.bass as bass
from concourse import mybir

P = 128
B, F, D, H = 1024, 39, 16, 128
TILES = B // P
GB = P // D
GPT = P // GB
SHIFTS = (F + 1) // 2
WRAP = F + SHIFTS - 1
SPK = P // F
KR = SPK * F
KT = -(-SHIFTS // SPK)
KLAST = (SHIFTS - (KT - 1) * SPK) * F
QG = 4
QUARTERS = GPT // QG
QC = QG * P
LAYOUTS = SHIFTS + SPK
NDENSE, N1, N2 = 16, 512, 256
SPARE = 64
FJ = F + 1
JC = 4
CHUNKS = -(-F // JC)
DVE_CHUNKS = [1, 4, 6, 9]
ACT_CHUNKS = [0, 2, 3, 5, 7, 8]
DC, AC = len(DVE_CHUNKS), len(ACT_CHUNKS)
ACT_BANKS = 3
SLOTS = 4
STEPS = F - AC * JC
RING = AC - 1
POOL_STEPS = RING - 1
OWN = 2 + JC
PARTS = OWN + JC
PAIR = 2
PPT = GPT // PAIR
ZLEAD, XLEAD = 4, 3
L0_PLACES = [(0, 4), (0, 5), (0, 6), (0, 8), (0, 9), (1, 0), (1, 1)]
X_F_LOADS = [(0, F), (F, 16), (F + 16, WRAP - F - 16)]
XF = 16 * len(X_F_LOADS)
EARLY = 24
GATHER_PLACES = [1, 2, 4]

F32 = mybir.dt.float32
F32R = mybir.dt.float32r
I32 = mybir.dt.int32
ALU = mybir.AluOpType
ACT = mybir.ActivationFunctionType
AX_X = mybir.AxisListType.X


def wait(eng, sem, t, per_tile, n):
    if isinstance(t, int) and t * per_tile + n <= 0:
        return
    eng.wait_ge(sem, t * per_tile + n)


def chunk_j(c):
    start = JC * c - (c > DVE_CHUNKS[-1]) * (CHUNKS * JC - F)
    return range(start, start + JC - (c == DVE_CHUNKS[-1]) * (CHUNKS * JC - F))


def dve_steps(n):
    return n // DC * STEPS + n % DC * JC


def dlrm_cin_kernel(nc, tables, ids, dense_t, w0a, w0b, b0, w1_t, b1, w2_t, b2,
                    wt1, bt1, wt2, bt2, wt3, identity, spreads, row_mask, turned, out):
    ctx = ExitStack()
    with ctx:
        def sb(name, shape, dt=F32):
            return ctx.enter_context(nc.sbuf_tensor(name, shape, dt))

        def pb(name):
            return ctx.enter_context(nc.psum_tensor(name, [P, 512], F32))

        def sem(name):
            return ctx.enter_context(nc.semaphore(name))

        w1_hi = sb("w1_hi", [P, F * H], F32R)
        w1_lo = sb("w1_lo", [P, F * H], F32R)
        w2 = sb("w2", [P, F, H])
        w0_hi = sb("w0_hi", [KR, KT, H], F32R)
        w0_lo = sb("w0_lo", [KR, KT, H], F32R)
        wt1_z = sb("wt1_z", [P, 3, N1])
        wt2_sb = sb("wt2_sb", [P, N1 // P, N2])
        wt3_sb = sb("wt3_sb", [P, N2 // P])
        bt1_sb = sb("bt1_sb", [P, N1 // P])
        bt2_sb = sb("bt2_sb", [P, N2 // P])
        b0_sb = sb("b0_sb", [P, 1])
        b0_16 = sb("b0_16", [P, 1])
        b1_rows = sb("b1_rows", [P, H])
        b2_sb = sb("b2_sb", [P, 1])
        b2_16 = sb("b2_16", [P, 1])
        ident = sb("ident", [P, P])
        mask = sb("mask", [P, GB])
        ids_tile = sb("ids_tile", [P, F], I32)
        emb = sb("emb", [P, WRAP * D])
        x_f = sb("x_f", [P, P, D])
        x_bd = sb("x_bd", [P, GPT, F])
        x_now = sb("x_now", [P, 4, FJ])
        x_same = sb("x_same", [P, 2, QC])
        x_shift = sb("x_shift", [P, 2, KT, QC])
        z = sb("z", [P, KT, P])
        z_hi = sb("z_hi", [P, 2, KT, PAIR * P], F32R)
        z_lo = sb("z_lo", [P, 2, KT, PAIR * P], F32R)
        x1_hi = sb("x1_hi", [P, 4 * P], F32R)
        x1_lo = sb("x1_lo", [P, 4 * P], F32R)
        scaled = sb("scaled", [P, SLOTS, JC * H])
        w0_two = scaled[0:KR, :, :].rearrange("p s n -> p (s n)")[:, 0:2 * KT * H].rearrange(
            "p (a k h) -> p a k h", a=2, k=KT)
        parts = sb("parts", [P, 2, PARTS, H])
        spread = parts[0:WRAP, :, :, :].rearrange("f a p h -> f (a p h)")[:, 0:(KT + 1) * KR].rearrange(
            "f (n r) -> f n r", n=KT + 1)
        x2 = sb("x2", [P, 2, H])
        x_diag = sb("x_diag", [P, 2, GB, FJ])
        g_sb = sb("g_sb", [P, FJ, P])
        w1_raw = g_sb[:, 0:F, :].rearrange("k j h -> k (j h)")
        z_first = w1_raw[:, 0:KT * P].rearrange("p (k n) -> p k n", k=KT)
        res0 = sb("res0", [P, P])
        z_top = sb("z_top", [P, 3, P])
        h1 = sb("h1", [P, N1 // P, P])
        h2 = sb("h2", [P, N2 // P, P])
        spare = x_f[SPARE:SPARE + NDENSE, :, :].rearrange("p b d -> p (b d)")
        dense, wt1_dense, y_sb = spare[:, 0:P], spare[:, P:P + N1], spare[0:1, P + N1:P + N1 + P]

        y_act = [pb(f"y_act{n}") for n in range(ACT_BANKS)]
        y_dve = [pb("y_dve0"), pb("y_dve1")]
        cin0_bank = pb("cin0")
        cin0 = cin0_bank[:, 0:PAIR * P]
        g_ps = pb("g_ps")
        misc = pb("misc")
        one_banks = [misc, g_ps, y_act[0], y_act[1]]
        two_banks = [y_act[2], y_dve[0]]
        first_banks = [y_act[2], y_dve[0], y_dve[1], cin0_bank, *one_banks]

        s_ids = sem("ids_loaded")
        s_gather = sem("gathered")
        s_w1 = sem("w1_loaded")
        s_w0 = sem("w0_loaded")
        s_w2 = sem("w2_loaded")
        s_const = sem("consts_loaded")
        s_dense = sem("dense_loaded")
        s_top = sem("top_loaded")
        s_ones = sem("ones_set")
        s_w1hi = sem("w1_hi_made")
        s_w1lo = sem("w1_lo_made")
        s_w0sum = sem("w0_summed")
        s_w0hi = sem("w0_hi_made")
        s_w0lo = sem("w0_lo_made")
        s_zhi = sem("z_hi_made")
        s_zlo = sem("z_lo_made")
        s_bias = sem("biases_made")
        s_x_one = sem("first_x_transposed")
        s_xt = sem("x_transposed")
        s_turned = sem("x_turned_in_dram")
        s_xf = sem("x_f_written")
        s_xbd = sem("x_bd_written")
        s_z = sem("z_made")
        s_now = sem("x_now_made")
        s_wrap = sem("emb_wrapped")
        s_spread = sem("first_quarter_spread")
        s_first_act = sem("first_quarter_written_by_act")
        s_first_dve = sem("first_quarter_written_by_dve")
        s_lay = [sem("x_laid_out_even"), sem("x_laid_out_odd")]
        s_cin0 = sem("cin0_summed")
        s_x1hi = sem("x1_hi_made")
        s_x1lo = sem("x1_lo_made")
        s_res0 = sem("res0_made")
        s_yact = sem("y_for_act")
        s_ydve = sem("y_for_dve")
        s_scaled = sem("scaled")
        s_steps = sem("dve_steps")
        s_pool = sem("pool_steps")
        s_x2 = sem("x2_made")
        s_diag = sem("x_diag_made")
        s_g = sem("g_summed")
        s_gc = sem("g_written")
        s_cin2 = sem("cin2_summed")
        s_ztop0 = sem("z_top0_made")
        s_ztop1 = sem("z_top1_made")
        s_ztop2 = sem("z_top2_made")
        s_h1p = sem("h1_summed")
        s_h1 = sem("h1_made")
        s_h2p = sem("h2_summed")
        s_h2 = sem("h2_made")
        s_yp = sem("y_summed")
        s_y = sem("y_made")
        s_out = sem("y_stored")

        block = ctx.enter_context(nc.Block())

        def first_copy(copy, m, written):
            pair = m % (len(first_banks) // 2)
            cols = slice(m // (len(first_banks) // 2) * PAIR * P, (m // (len(first_banks) // 2) + 1) * PAIR * P)
            bank = first_banks[m][0:KR, :].rearrange("r (k n) -> r k n", k=2)
            if pair == 0:
                copy(x_same[0:KR, 0, cols], bank[:, 0, :])
                ins = copy(x_shift[0:KR, 0, 0, cols], bank[:, 1, :])
            else:
                ins = copy(x_shift[0:KR, 0, 2 * pair - 1:2 * pair + 1, cols], bank)
            ins.then_inc(written, 1)

        def tiles(eng, body):
            body(0, True, False)
            with eng.Fori(1, TILES - 1) as t:
                body(t, False, False)
            body(TILES - 1, False, True)

        @block.sync
        def _(sp):
            def load_ids(t, row=None):
                wait(sp, s_gather, t, 16 * F, 0)
                sp.dma_start(ids_tile[:, :], ids[bass.ds(t * P if row is None else row, P), :]).then_inc(s_ids, 16)

            load_ids(0)
            sp.dma_start(ident[:, :], identity).then_inc(s_const, 16)
            sp.dma_start(mask[:, :], row_mask).then_inc(s_const, 16)
            sp.dma_start(b0_sb[:, :], b0).then_inc(s_const, 16)
            sp.dma_start(b2_sb[:, :], b2).then_inc(s_const, 16)
            sp.dma_start(b1_rows[:, :], bass.AP(b1.tensor, 0, [[0, P], [1, H]])).then_inc(s_const, 16)
            sp.dma_start(spread, spreads).then_inc(s_const, 16)
            sp.dma_start(w0_two[:, 0], w0a).then_inc(s_w0, 16)
            sp.dma_start(w0_two[:, 1], w0b).then_inc(s_w0, 16)
            sp.dma_start(w1_raw, w1_t).then_inc(s_w1, 16)
            sp.dma_start(w2[:, :, :], w2_t).then_inc(s_w2, 16)
            sp.dma_start(wt1_z[:, :, :], wt1[0:3 * H, :].rearrange("(l p) n -> p l n", p=P)).then_inc(s_top, 16)
            sp.dma_start(wt1_dense, wt1[3 * H:3 * H + NDENSE, :]).then_inc(s_top, 16)
            sp.dma_start(wt2_sb[:, :, :], wt2.rearrange("(l p) n -> p l n", p=P)).then_inc(s_top, 16)
            sp.dma_start(wt3_sb[:, :], wt3).then_inc(s_top, 16)
            sp.dma_start(bt1_sb[:, :], bt1).then_inc(s_top, 16)
            sp.dma_start(bt2_sb[:, :], bt2).then_inc(s_top, 16)

            def lay_out(t, q):
                wait(sp, s_z, t, GPT, QG * (q - 1))
                if q == 0:
                    wait(sp, s_xf, t, XF, XF)
                cols = x_f[:, :, :].rearrange("f b d -> f (b d)")[:, q * QC:(q + 1) * QC]
                for k in range(SPK):
                    sp.dma_start(x_same[k * F:(k + 1) * F, q % 2, :], cols[0:F, :]).then_inc(s_lay[q % 2], 16)
                for s in range(SHIFTS):
                    row = s % SPK * F
                    sp.dma_start(x_shift[row:row + F, q % 2, s // SPK, :], cols[s:s + F, :]).then_inc(s_lay[q % 2], 16)

            def x_f_layout(t, ids_row=None):
                wait(sp, s_gather, t, 16 * F, 16 * F)
                sp.dma_start(turned.rearrange("f b d -> b f d"),
                             emb[:, 0:F * D].rearrange("b (f d) -> b f d", d=D)).then_inc(s_turned, 16)
                wait(sp, s_lay[0], t, 16 * LAYOUTS * QUARTERS // 2, -16 * LAYOUTS)
                load_ids(t + 1, ids_row)
                wait(sp, s_turned, t, 16, 0)
                wait(sp, s_lay[1], t, 16 * LAYOUTS * QUARTERS // 2, 0)
                for f0, n in X_F_LOADS:
                    sp.dma_start(x_f[f0:f0 + n, :, :], turned[f0 % F:f0 % F + n, :, :]).then_inc(s_xf, 16)

            def store(t, row=None):
                wait(sp, s_y, t, 1, 1)
                sp.dma_start(out[:, bass.ds(t * P if row is None else row, P)], y_sb).then_inc(s_out, 16)

            def load_dense(t, row=None):
                wait(sp, s_h1p, t, 1, 0)
                sp.dma_start(dense, dense_t[:, bass.ds(t * P if row is None else row, P)]).then_inc(s_dense, 16)

            def body(t, first, last):
                ids_row = out_row = row = None
                if not first and not last:
                    ids_row, out_row, row = sp.snap((t + 2) * P), sp.snap((t - 1) * P), sp.snap(t * P)
                lay_out(t, 2)
                if not first:
                    store(t - 1, out_row)
                lay_out(t, 3)
                load_dense(t, row)
                if not last:
                    x_f_layout(t + 1, ids_row)
                    lay_out(t + 1, 0)
                    lay_out(t + 1, 1)

            load_ids(1)
            sp.wait_ge(s_ones, 2)
            sp.wait_ge(s_xf, XF)
            lay_out(0, 1)
            tiles(sp, body)
            store(TILES - 1)
            sp.wait_ge(s_out, 16 * TILES)

        @block.gpsimd
        def _(pool):
            def gather(t, fields):
                for f in fields:
                    nc.gpsimd.indirect_dma_start(
                        out=emb[:, f * D:(f + 1) * D], out_offset=None, in_=tables[f],
                        in_offset=bass.IndirectOffsetOnAxis(ap=ids_tile[:, f:f + 1], axis=0),
                    ).then_inc(s_gather, 16)

            def gather_waits(t):
                wait(pool, s_ids, t, 16, 16)
                if isinstance(t, int) and t == 1:
                    pool.wait_ge(s_x_one, 4)
                wait(pool, s_turned, t, 16, -16)

            def add(t, n, out_, a, b):
                wait(pool, s_pool, t, GPT * POOL_STEPS, n)
                nc.gpsimd.tensor_tensor(out_, a, b, ALU.add).then_inc(s_pool, 1)

            def body(t, first, last):
                for i in range(GPT):
                    total = parts[:, i % 2, 2:OWN, :].rearrange("p s h -> p (s h)")
                    if i == GPT - EARLY // 3 and not last:
                        gather_waits(t + 2)
                    wait(pool, s_x2, t, GPT, i - 1)
                    for m in range(1, RING):
                        wait(pool, s_scaled, t, GPT * AC, AC * i + m + 1)
                        slot = (RING * i + m) % SLOTS
                        add(t, POOL_STEPS * i + m - 1, total,
                            scaled[:, (slot - 1) % SLOTS, :] if m == 1 else total, scaled[:, slot, :])
                        if m in GATHER_PLACES and not last:
                            n = GATHER_PLACES.index(m)
                            if i < (F - EARLY) // 3:
                                gather(t + 1, [EARLY + 3 * i + n])
                            if i >= GPT - EARLY // 3:
                                gather(t + 2, [3 * (i - GPT + EARLY // 3) + n])

            gather_waits(0)
            gather(0, range(F))
            gather_waits(1)
            gather(1, range(EARLY))
            tiles(pool, body)

        @block.scalar
        def _(act):
            def x_f_copy(a):
                act.wait_ge(s_x_one, a + 1)
                nc.scalar.copy(x_f[0:WRAP, :, 4 * a:4 * a + 4].rearrange("f b d -> f d b"),
                               one_banks[a][0:WRAP, 0:4 * P].rearrange("f (d b) -> f d b", d=4)).then_inc(s_xf, XF // 4)

            def z_high(t, i, z=z):
                wait(act, s_cin0, t, PPT, i // PAIR - 1)
                wait(act, s_z, t, GPT, i + 1)
                c = i % PAIR * P
                nc.scalar.copy(z_hi[0:KR, i // PAIR % 2, :, c:c + P], z[0:KR, :, :]).then_inc(s_zhi, 1)

            def x1_high(t, pair):
                wait(act, s_yact, t, GPT * AC, PAIR * AC * (pair - 1))
                wait(act, s_cin0, t, PPT, pair + 1)
                c = pair % 2 * PAIR * P
                nc.scalar.activation(x1_hi[:, c:c + PAIR * P], cin0, ACT.Identity, bias=b0_sb[:, 0:1]).then_inc(s_x1hi, 1)

            def g_copy(t, i):
                wait(act, s_g, t, GPT, i + 1)
                if i == 0:
                    wait(act, s_cin2, t, 1, 0)
                    wait(act, s_ztop1, t, 1, 0)
                nc.scalar.copy(g_sb[:, :, GB * i:GB * i + GB].rearrange("k j b -> k b j"),
                               g_ps[:, 0:GB * FJ].rearrange("k (b j) -> k b j", b=GB)).then_inc(s_gc, 1)

            def scale(t, i, m):
                c = ACT_CHUNKS[m]
                wait(act, s_yact, t, GPT * AC, AC * i + m + 1)
                if m < RING:
                    q = RING * i + m - SLOTS
                    n = POOL_STEPS * (q // RING) + max(q % RING - 1, 0) + 1
                    wait(act, s_pool, t, GPT * POOL_STEPS, n)
                    to = scaled[:, (RING * i + m) % SLOTS, :]
                else:
                    wait(act, s_x2, t, GPT, i - 1)
                    to = parts[:, i % 2, OWN:PARTS, :].rearrange("p s h -> p (s h)")
                for k, j in enumerate(chunk_j(c)):
                    ins = nc.scalar.activation(to[:, k * H:(k + 1) * H],
                                               y_act[(AC * i + m) % ACT_BANKS][:, k * H:(k + 1) * H], ACT.Copy,
                                               scale=x_now[:, i % 4, j:j + 1])
                ins.then_inc(s_scaled, 1)

            def res1_copy(t):
                wait(act, s_gc, t, GPT, GPT)
                wait(act, s_h1p, t, 1, 0)
                nc.scalar.copy(z_top[:, 1, :], g_sb[:, F, :]).then_inc(s_ztop1, 1)

            def res2_copy(t):
                wait(act, s_cin2, t, 1, 1)
                nc.scalar.activation(z_top[:, 2, :], misc[:, 0:P], ACT.Identity, bias=b2_16[:, 0:1]).then_inc(s_ztop2, 1)

            def relu1(t):
                wait(act, s_h1p, t, 1, 1)
                wait(act, s_h2p, t, 1, 0)
                for m in range(N1 // P):
                    ins = nc.scalar.activation(h1[:, m, :], misc[:, m * P:(m + 1) * P], ACT.Relu, bias=bt1_sb[:, m:m + 1])
                ins.then_inc(s_h1, 1)

            def relu2(t):
                wait(act, s_h2p, t, 1, 1)
                wait(act, s_yp, t, 1, 0)
                for m in range(N2 // P):
                    ins = nc.scalar.activation(h2[:, m, :], misc[:, m * P:(m + 1) * P], ACT.Relu, bias=bt2_sb[:, m:m + 1])
                ins.then_inc(s_h2, 1)

            def y_copy(t):
                wait(act, s_yp, t, 1, 1)
                wait(act, s_out, t, 16, 0)
                nc.scalar.copy(y_sb, misc[0:1, 0:P]).then_inc(s_y, 1)

            def body(t, first, last):
                for i in range(GPT):
                    wait(act, s_now, t, GPT, i + 1)
                    for m in range(AC):
                        scale(t, i, m)
                        if m == 1 and i % PAIR == PAIR - 1 and not (last and i + 1 >= GPT):
                            x1_high(t, (i + 1) // PAIR)
                        if m == 2:
                            if i > 1:
                                g_copy(t, i - 2)
                            elif not first:
                                g_copy(t - 1, GPT - 2 + i)
                        if m == 3 and not (last and i + ZLEAD >= GPT):
                            z_high(t, i + ZLEAD)
                    if not first:
                        if i == 1:
                            res1_copy(t - 1)
                            res2_copy(t - 1)
                        if i == 2:
                            relu1(t - 1)
                        if i == 3:
                            relu2(t - 1)
                        if i == 4:
                            y_copy(t - 1)

            act.wait_ge(s_w0sum, 1)
            nc.scalar.copy(w0_hi[:, :, :], w0_two[:, 0]).then_inc(s_w0hi, 1)
            act.wait_ge(s_w1, 16)
            nc.scalar.copy(w1_hi[:, :], w1_raw).then_inc(s_w1hi, 1)
            for a in range(4):
                x_f_copy(a)
            act.wait_ge(s_const, 16 * 6)
            for i in range(0, ZLEAD, PAIR):
                for m in range(2 * i, 2 * i + 2 * PAIR, 2):
                    act.wait_ge(s_spread, m + 1)
                    first_copy(nc.scalar.copy, m, s_first_act)
                z_high(0, i)
                if i == PAIR:
                    x1_high(0, 0)
                z_high(0, i + 1, z_first)
            act.wait_ge(s_top, 16 * 6)
            act.wait_ge(s_bias, 2)
            act.wait_ge(s_w1lo, 1)
            act.wait_ge(s_w0lo, 1)
            tiles(act, body)
            g_copy(TILES - 1, GPT - 2)
            g_copy(TILES - 1, GPT - 1)
            res1_copy(TILES - 1)
            res2_copy(TILES - 1)
            relu1(TILES - 1)
            relu2(TILES - 1)
            y_copy(TILES - 1)

        @block.vector
        def _(dve):
            def x_bd_copy(t, half, bank=misc):
                wait(dve, s_xt, t, 2, 1 + half)
                g0 = half * GPT // 2
                wait(dve, s_now, t, GPT, g0 - GPT // 2)
                src = bank[:, 0:GPT // 2 * F].rearrange("p (g f) -> p g f", f=F)
                nc.vector.tensor_copy(x_bd[:, g0:g0 + GPT // 2, :], src).then_inc(s_xbd, 1)

            def wrap():
                dve.wait_ge(s_gather, 16 * F)
                nc.vector.tensor_copy(emb[:, F * D:WRAP * D], emb[:, 0:(WRAP - F) * D]).then_inc(s_wrap, 1)

            def products(t, i, z=z):
                q = i // QG
                wait(dve, s_lay[q % 2], t, 16 * LAYOUTS * QUARTERS // 2, 16 * LAYOUTS * (q // 2 + q % 2))
                if z is not z_first:
                    wait(dve, s_zhi, t, GPT, i)
                    wait(dve, s_zlo, t, GPT, i)
                cols = slice(i % QG * P, (i % QG + 1) * P)
                nc.vector.tensor_tensor(z[0:KR, :, :], x_same[0:KR, q % 2, cols].unsqueeze(1).broadcast_to([KR, KT, P]),
                                        x_shift[0:KR, q % 2, :, cols], ALU.mult).then_inc(s_z, 1)

            def z_low(t, i, z=z):
                wait(dve, s_cin0, t, PPT, i // PAIR - 1)
                wait(dve, s_zhi, t, GPT, i + 1)
                pair, c = i // PAIR % 2, i % PAIR * P
                nc.vector.tensor_tensor(z_lo[0:KR, pair, :, c:c + P], z[0:KR, :, :],
                                        z_hi[0:KR, pair, :, c:c + P].bitcast(F32), ALU.subtract).then_inc(s_zlo, 1)

            def x_now_copy(t, i):
                g = i % GPT
                wait(dve, s_xbd, t, 2, 2 * (i // GPT) + (1 if g < GPT // 2 else 2))
                wait(dve, s_scaled, t, GPT * AC, AC * (i - 3))
                wait(dve, s_steps, t, GPT * STEPS, STEPS * (i - 3))
                wait(dve, s_diag, t, GPT, i - 3)
                nc.vector.tensor_copy(x_now[:, i % 4, 0:F], x_bd[:, g, 0:F]).then_inc(s_now, 1)

            def res0_sum(t, pair):
                if pair % PPT == 0:
                    wait(dve, s_ztop0, t, 1, pair // PPT)
                wait(dve, s_x1hi, t, PPT, pair + 1)
                b = pair % PPT * PAIR * GB
                nc.vector.tensor_reduce(res0[:, b:b + PAIR * GB], cin0.rearrange("h (b d) -> h b d", d=D),
                                        AX_X, ALU.add).then_inc(s_res0, 1)

            def x1_low(t, pair):
                wait(dve, s_x1hi, t, PPT, pair + 1)
                wait(dve, s_yact, t, GPT * AC, PAIR * AC * (pair - 1))
                c = pair % 2 * PAIR * P
                nc.vector.scalar_tensor_tensor(out=x1_lo[:, c:c + PAIR * P], in0=cin0, scalar=b0_sb[:, 0:1],
                                               in1=x1_hi[:, c:c + PAIR * P].bitcast(F32), op0=ALU.add,
                                               op1=ALU.subtract).then_inc(s_x1lo, 1)

            def multiply_add(t, i, m):
                wait(dve, s_ydve, t, GPT * DC, DC * i + m + 1)
                bank = y_dve[(DC * i + m) % 2]
                for k, j in enumerate(chunk_j(DVE_CHUNKS[m])):
                    n = JC * m + k
                    acc = parts[:, i % 2, n % 2, :]
                    y = bank[:, k * H:(k + 1) * H]
                    x = x_now[:, i % 4, j:j + 1]
                    wait(dve, s_steps, t, GPT * STEPS, STEPS * i + n - 1)
                    if n == 0:
                        wait(dve, s_x2, t, GPT, i - 1)
                    if n == 1:
                        ins = nc.vector.tensor_scalar(acc, y, x, None, ALU.mult)
                    else:
                        ins = nc.vector.scalar_tensor_tensor(out=acc, in0=y, scalar=x,
                                                             in1=b1_rows[:, :] if n == 0 else acc,
                                                             op0=ALU.mult, op1=ALU.add)
                    ins.then_inc(s_steps, 1)

            def x2_sum(t, i):
                wait(dve, s_scaled, t, GPT * AC, AC * (i + 1))
                wait(dve, s_pool, t, GPT * POOL_STEPS, POOL_STEPS * (i + 1))
                wait(dve, s_steps, t, GPT * STEPS, STEPS * (i + 1))
                wait(dve, s_g, t, GPT, i - 1)
                nc.vector.tensor_reduce(x2[:, i % 2, :], parts[:, i % 2, :, :].rearrange("p s h -> p h s"), AX_X,
                                        ALU.add).then_inc(s_x2, 1)

            def x_diagonal(t, i):
                wait(dve, s_g, t, GPT, i - 1)
                nc.vector.tensor_tensor(x_diag[:, i % 2, :, :], mask[:, :].unsqueeze(2).broadcast_to([P, GB, FJ]),
                                        x_now[:, i % 4, :].unsqueeze(1).broadcast_to([P, GB, FJ]),
                                        ALU.mult).then_inc(s_diag, 1)

            def body(t, first, last):
                for i in range(GPT):
                    wait(dve, s_now, t, GPT, i + 1)
                    multiply_add(t, i, 0)
                    if not (last and i + ZLEAD >= GPT):
                        products(t, i + ZLEAD)
                    multiply_add(t, i, 1)
                    if i % PAIR == PAIR - 1 and not (last and i + 1 >= GPT):
                        x1_low(t, (i + 1) // PAIR)
                    x_diagonal(t, i)
                    multiply_add(t, i, 2)
                    if i > 0:
                        x2_sum(t, i - 1)
                    elif not first:
                        x2_sum(t - 1, GPT - 1)
                    if i == GPT - 1:
                        wait(dve, s_res0, t, PPT, PPT)
                        wait(dve, s_h1p, t, 1, 0)
                        nc.vector.tensor_scalar(z_top[:, 0, :], res0[:, :], b0_16[:, 0:1], None,
                                                ALU.add).then_inc(s_ztop0, 1)
                    if i % PAIR == PAIR - 1 and not (last and i + 1 >= GPT):
                        res0_sum(t, (i + 1) // PAIR)
                    multiply_add(t, i, 3)
                    if not (last and i + ZLEAD >= GPT):
                        z_low(t, i + ZLEAD)
                    if not (last and i + XLEAD >= GPT):
                        x_now_copy(t, i + XLEAD)
                    if not last and i in (11, 13):
                        x_bd_copy(t + 1, int(i == 13))

            nc.vector.memset(x_now[:, :, F:FJ], 1.0).then_inc(s_ones, 1)
            nc.vector.memset(x_shift[:, :, KT - 1, :], 0.0).then_inc(s_ones, 1)
            dve.wait_ge(s_const, 16 * 6)
            nc.vector.tensor_scalar(b0_16[:, :], b0_sb[:, :], float(D), None, ALU.mult).then_inc(s_bias, 1)
            nc.vector.tensor_scalar(b2_16[:, :], b2_sb[:, :], float(D), None, ALU.mult).then_inc(s_bias, 1)
            dve.wait_ge(s_w0, 32)
            nc.vector.tensor_tensor(w0_two[:, 0], w0_two[:, 0], w0_two[:, 1], ALU.add).then_inc(s_w0sum, 1)
            dve.wait_ge(s_w0hi, 1)
            nc.vector.tensor_tensor(w0_lo[:, :, :], w0_two[:, 0], w0_hi[:, :, :].bitcast(F32),
                                    ALU.subtract).then_inc(s_w0lo, 1)
            dve.wait_ge(s_w1hi, 1)
            nc.vector.tensor_tensor(w1_lo[:, :], w1_raw, w1_hi[:, :].bitcast(F32),
                                    ALU.subtract).then_inc(s_w1lo, 1)
            wrap()
            for i in range(0, ZLEAD, PAIR):
                for m in range(2 * i + 1, 2 * i + 2 * PAIR, 2):
                    dve.wait_ge(s_spread, m + 1)
                    first_copy(nc.vector.tensor_copy, m, s_first_dve)
                dve.wait_ge(s_first_act, i + PAIR)
                dve.wait_ge(s_first_dve, i + PAIR)
                products(0, i)
                if i == PAIR:
                    dve.wait_ge(s_zhi, PAIR)
                    dve.wait_ge(s_zlo, PAIR)
                products(0, i + 1, z_first)
                z_low(0, i)
                if i == PAIR:
                    x1_low(0, 0)
                    res0_sum(0, 0)
                    for half in range(2):
                        x_bd_copy(0, half, two_banks[half])
                    for n in range(XLEAD):
                        x_now_copy(0, n)
                z_low(0, i + 1, z_first)
            dve.wait_ge(s_bias, 2)
            dve.wait_ge(s_ones, 2)
            tiles(dve, body)
            x2_sum(TILES - 1, GPT - 1)

        @block.tensor
        def _(pe):
            def x_two_waits(t, half):
                wait(pe, s_xf, t, XF, XF)
                if half == 0:
                    wait(pe, s_y, t, 1, -1)
                if half == 1:
                    wait(pe, s_xbd, t, 2, 1)

            def x_stage_one(a):
                for k in range(4):
                    d = 4 * a + k
                    ins = nc.tensor.transpose(one_banks[a][0:WRAP, k * P:(k + 1) * P],
                                              emb[:, :].rearrange("p (f d) -> p f d", d=D)[:, :, d], ident[:, :])
                ins.then_inc(s_x_one, 1)

            def x_stage_two(t, half, bank=misc):
                for k in range(GPT // 2):
                    g = half * GPT // 2 + k
                    ins = nc.tensor.transpose(bank[:, k * F:(k + 1) * F], x_f[0:F, GB * g:GB * g + GB, :],
                                              ident[0:F, 0:F])
                ins.then_inc(s_xt, 1)

            def first_fill(m):
                pair, half = m % (len(first_banks) // 2), m // (len(first_banks) // 2)
                b = slice(half * PAIR * GB, (half + 1) * PAIR * GB)
                for k in range(2):
                    ins = nc.tensor.matmul(first_banks[m][0:KR, k * PAIR * P:(k + 1) * PAIR * P],
                                           spread[:, 2 * pair + k, :], x_f[0:WRAP, b, :], start=True, stop=True)
                ins.then_inc(s_spread, 1)

            def layer0(t, pair, k):
                if k == 0:
                    wait(pe, s_zlo, t, GPT, PAIR * pair + PAIR)
                    wait(pe, s_x1lo, t, PPT, pair)
                    wait(pe, s_res0, t, PPT, pair)
                rows = KR if k < KT - 1 else KLAST
                for n, (w, x) in enumerate(((w0_hi, z_hi), (w0_lo, z_hi), (w0_hi, z_lo))):
                    ins = nc.tensor.matmul(cin0, w[0:rows, k, :], x[0:rows, pair % 2, k, :],
                                           start=(k == 0 and n == 0), stop=(k == KT - 1 and n == 2))
                if k == KT - 1:
                    ins.then_inc(s_cin0, 1)

            def layer1_chunk(t, i, c):
                if c == 0:
                    wait(pe, s_x1lo, t, PPT, i // PAIR + 1)
                if c in ACT_CHUNKS:
                    n = AC * i + ACT_CHUNKS.index(c)
                    bank, ready = y_act[n % ACT_BANKS], s_yact
                    wait(pe, s_scaled, t, GPT * AC, n + 1 - ACT_BANKS)
                else:
                    n = DC * i + DVE_CHUNKS.index(c)
                    bank, ready = y_dve[n % 2], s_ydve
                    wait(pe, s_steps, t, GPT * STEPS, dve_steps(n - 1))
                lo, hi = chunk_j(c)[0] * H, (chunk_j(c)[-1] + 1) * H
                for p, (x, w) in enumerate(((x1_hi, w1_hi), (x1_hi, w1_lo), (x1_lo, w1_hi))):
                    ins = nc.tensor.matmul(bank[:, 0:hi - lo], x[:, i % 4 * P:(i % 4 + 1) * P], w[:, lo:hi],
                                           start=(p == 0), stop=(p == 2))
                ins.then_inc(ready, 1)

            def g_matmul(t, i):
                wait(pe, s_x2, t, GPT, i + 1)
                wait(pe, s_gc, t, GPT, i)
                nc.tensor.matmul(g_ps[:, 0:GB * FJ], x2[:, i % 2, :], x_diag[:, i % 2, :, :],
                                 start=True, stop=True).then_inc(s_g, 1)

            def layer2(t, js, last=False):
                for j in js:
                    if j == 0:
                        wait(pe, s_gc, t, GPT, GPT)
                        wait(pe, s_y, t, 1, 0)
                        wait(pe, s_xbd, t, 2, 2 if last else 4)
                    ins = nc.tensor.matmul(misc[:, 0:P], w2[:, j, :], g_sb[:, j, :], start=(j == 0), stop=(j == F - 1))
                    if j == F - 1:
                        ins.then_inc(s_cin2, 1)

            def top1(t, m):
                if m == 0:
                    wait(pe, s_dense, t, 16, 16)
                    wait(pe, s_ztop0, t, 1, 1)
                    wait(pe, s_ztop1, t, 1, 1)
                    wait(pe, s_ztop2, t, 1, 1)
                for k in range(3):
                    nc.tensor.matmul(misc[:, m * P:(m + 1) * P], wt1_z[:, k, m * P:(m + 1) * P], z_top[:, k, :],
                                     start=(k == 0), stop=False)
                ins = nc.tensor.matmul(misc[:, m * P:(m + 1) * P], wt1_dense[:, m * P:(m + 1) * P],
                                       dense, start=False, stop=True)
                if m == N1 // P - 1:
                    ins.then_inc(s_h1p, 1)

            def top2(t, m):
                wait(pe, s_h1, t, 1, 1)
                for k in range(N1 // P):
                    ins = nc.tensor.matmul(misc[:, m * P:(m + 1) * P], wt2_sb[:, k, m * P:(m + 1) * P], h1[:, k, :],
                                           start=(k == 0), stop=(k == N1 // P - 1))
                if m == N2 // P - 1:
                    ins.then_inc(s_h2p, 1)

            def top3(t):
                wait(pe, s_h2, t, 1, 1)
                for k in range(N2 // P):
                    ins = nc.tensor.matmul(misc[0:1, 0:P], wt3_sb[:, k:k + 1], h2[:, k, :],
                                           start=(k == 0), stop=(k == N2 // P - 1))
                ins.then_inc(s_yp, 1)

            def body(t, first, last):
                for i in range(GPT):
                    for c in range(CHUNKS):
                        if not last and i in (11, 13) and c == 6:
                            x_two_waits(t + 1, int(i == 13))
                        layer1_chunk(t, i, c)
                        if (i % PAIR, c) in L0_PLACES and not (last and i + PAIR >= GPT):
                            layer0(t, i // PAIR + 1, L0_PLACES.index((i % PAIR, c)))
                        if c == 2:
                            if i > 1:
                                g_matmul(t, i - 2)
                            elif not first:
                                g_matmul(t - 1, GPT - 2 + i)
                        if not first:
                            if i == 1 and c >= 6:
                                layer2(t - 1, range(10 * (c - 6), min(10 * (c - 6) + 10, F)))
                            if i == 2 and c in (4, 5, 6, 8):
                                top1(t - 1, (4, 5, 6, 8).index(c))
                            if i == 3 and c in (5, 6):
                                top2(t - 1, c - 5)
                            if i == 4 and c == 5:
                                top3(t - 1)
                        if not last:
                            if i in (11, 13) and c == 6:
                                x_stage_two(t + 1, int(i == 13))

            pe.wait_ge(s_const, 16 * 6)
            pe.wait_ge(s_gather, 16 * F)
            pe.wait_ge(s_wrap, 1)
            for a in range(4):
                x_stage_one(a)
            pe.wait_ge(s_xf, XF)
            for m in range(len(first_banks)):
                first_fill(m)
            pe.wait_ge(s_w0lo, 1)
            pe.wait_ge(s_first_dve, 2)
            for k in range(KT):
                layer0(0, 0, k)
            pe.wait_ge(s_first_act, 1)
            for half in range(2):
                x_stage_two(0, half, two_banks[half])
            pe.wait_ge(s_first_act, len(first_banks) // 2)
            pe.wait_ge(s_first_dve, len(first_banks) // 2)
            pe.wait_ge(s_xbd, 2)
            pe.wait_ge(s_w1lo, 1)
            pe.wait_ge(s_w2, 16)
            pe.wait_ge(s_top, 16 * 6)
            tiles(pe, body)
            g_matmul(TILES - 1, GPT - 2)
            g_matmul(TILES - 1, GPT - 1)
            layer2(TILES - 1, range(F), last=True)
            for m in range(N1 // P):
                top1(TILES - 1, m)
            for m in range(N2 // P):
                top2(TILES - 1, m)
            top3(TILES - 1)


def kernel(**inputs):
    import numpy as np
    import concourse.bacc as bacc
    from concourse.bass_utils import run_bass_kernel_spmd

    nc = bacc.Bacc("TRN2", target_bir_lowering=False, num_devices=1)
    a = {k: np.asarray(v) for k, v in inputs.items()}

    w0 = np.concatenate([a["L0_rec_W0"], np.zeros((H, 1), np.float32)], axis=1)
    zero = F * F
    i1 = np.tile(np.arange(F), SHIFTS)
    i2 = (i1 + np.repeat(np.arange(SHIFTS), F)) % F
    order_a, order_b = np.full(KT * KR, zero), np.full(KT * KR, zero)
    order_a[:len(i1)] = i1 * F + i2
    order_b[:len(i1)] = np.where(i1 == i2, zero, i2 * F + i1)

    spreads = np.zeros((WRAP, KT + 1, KR), np.float32)
    spreads[i1[:KR], 0, np.arange(KR)] = 1
    for shift in range(SHIFTS):
        for i in range(F):
            spreads[i + shift, 1 + shift // SPK, shift % SPK * F + i] = 1

    def pair_rows(order):
        return np.ascontiguousarray(w0[:, order].T.reshape(KT, KR, H).transpose(1, 0, 2))

    def by_k(w):
        return w.reshape(H, F, H).transpose(2, 1, 0)

    arrays = {f"tbl_{f}": a[f"tbl_{f}"] for f in range(F)}
    arrays |= {
        "ids": np.concatenate([a["ids"], a["ids"][:P]]),
        "dense_t": a["dense_ctx"].T,
        "w0a": pair_rows(order_a), "w0b": pair_rows(order_b), "b0": a["L0_rec_b0"].reshape(H, 1),
        "w1_t": by_k(a["L0_rec_W1"]).reshape(H, F * H), "b1": a["L0_rec_b1"],
        "w2_t": by_k(a["L0_rec_W2"]), "b2": a["L0_rec_b2"].reshape(H, 1),
        "wt1": a["W_top1"], "bt1": a["b_top1"].reshape(N1 // P, P).T,
        "wt2": a["W_top2"], "bt2": a["b_top2"].reshape(N2 // P, P).T,
        "wt3": a["W_top3"].reshape(N2 // P, P).T,
        "identity": np.eye(P, dtype=np.float32),
        "spreads": spreads,
        "row_mask": np.repeat(np.eye(GB, dtype=np.float32), D, axis=0),
    }
    arrays = {f"in_{k}": np.ascontiguousarray(v) for k, v in arrays.items()}
    args = [nc.dram_tensor(k, v.shape, mybir.dt.from_np(v.dtype), kind="ExternalInput").ap() for k, v in arrays.items()]
    out = nc.dram_tensor("out_y", (1, B), F32, kind="ExternalOutput").ap()
    turned = nc.dram_tensor("turned", (F, P, D), F32, kind="Internal").ap()
    dlrm_cin_kernel(nc, args[:F], *args[F:], turned, out)
    r = run_bass_kernel_spmd(nc, [arrays], core_ids=[0])
    return r.results[0]["out_y"].reshape(B, 1)
```
